# Optimizing a Trainium2 kernel written in Bass

```python
import numpy as np
import jax
import jax.numpy as jnp

def _softmax(x, axis=-1):
    return jax.nn.softmax(x, axis=axis)

def _gelu(x):
    return jax.nn.gelu(x, approximate=True)

def _silu(x):
    return jax.nn.silu(x)

def _sigmoid(x):
    return jax.nn.sigmoid(x)

def _layernorm(x, axis=-1, eps=1e-05):
    m = jnp.mean(x, axis=axis, keepdims=True)
    v = jnp.var(x, axis=axis, keepdims=True)
    return (x - m) / jnp.sqrt(v + eps)

def _scatter_add(tgt, idx, src, axis=0):
    return tgt.at[idx].add(src)

def _segment_sum(src, seg, n):
    return jax.ops.segment_sum(src, seg, n)
kernel_name = 'mk_gnn_preln_d1_gnn_r8_3a1a56'

def setup_inputs(seed: int=0):
    np.random.seed(seed)
    _w = jnp.asarray

    def _rec_inputs():
        import jax
        import jax.numpy as jnp
        _gk = jax.random.key(seed)
        x = -0.0009044 + 1 * jax.random.normal(jax.random.fold_in(_gk, 1), (12500, 32), jnp.float32)
        src = jax.random.randint(jax.random.fold_in(_gk, 2), (400000,), 0, 12500, jnp.int32)
        dst = jax.random.randint(jax.random.fold_in(_gk, 3), (400000,), 0, 12500, jnp.int32)
        _o = jnp.argsort(dst, stable=True)
        src = src[_o]
        dst = dst[_o]
        edge_attr_32 = 0.000196303 + 1.00016 * jax.random.normal(jax.random.fold_in(_gk, 11), (400000, 32), jnp.float32)
        return (x, src, dst, edge_attr_32)
    x, src, dst, edge_attr_32 = _rec_inputs()

    def _L0_gnn_setup():
        import jax, jax.numpy as jnp
        import numpy as np
        N_NODES = 6250
        N_EDGES = 100000
        X_DIM = 32
        E_DIM = 32
        HID = 64
        OUT = 32
        key = jax.random.key(seed)
        ks = jax.random.split(key, 6)
        x = jax.random.normal(ks[0], (N_NODES, X_DIM), dtype=jnp.float32)
        edge_index = jax.random.randint(ks[1], (2, N_EDGES), 0, N_NODES, dtype=jnp.int64)
        edge_attr = jax.random.normal(ks[2], (N_EDGES, E_DIM), dtype=jnp.float32)
        in_dim = 2 * X_DIM + E_DIM
        W1 = jax.random.normal(ks[3], (in_dim, HID), dtype=jnp.float32) * (1.0 / np.sqrt(in_dim))
        b1 = jnp.zeros((HID,), dtype=jnp.float32)
        W2 = jax.random.normal(ks[4], (HID, OUT), dtype=jnp.float32) * (1.0 / np.sqrt(HID))
        b2 = jnp.zeros((OUT,), dtype=jnp.float32)
        return {'x': x, 'edge_index': edge_index, 'edge_attr': edge_attr, 'W1': W1, 'b1': b1, 'W2': W2, 'b2': b2}
    _L0_gnn_all = _L0_gnn_setup()
    _L0_gnn_in = {k: v for k, v in _L0_gnn_all.items() if k in ('W1', 'b1', 'W2', 'b2')}
    del _L0_gnn_all
    return {'x': x, 'src': src, 'dst': dst, 'edge_attr_32': edge_attr_32, 'L0_gnn_W1': _L0_gnn_in['W1'], 'L0_gnn_b1': _L0_gnn_in['b1'], 'L0_gnn_W2': _L0_gnn_in['W2'], 'L0_gnn_b2': _L0_gnn_in['b2']}

def reference(x, src, dst, edge_attr_32, L0_gnn_W1, L0_gnn_b1, L0_gnn_W2, L0_gnn_b2):
    import jax
    import jax.numpy as jnp

    def _L0_gnn_ref(x, edge_index, edge_attr, W1, b1, W2, b2):
        import jax, jax.numpy as jnp
        import numpy as np
        N_NODES = 6250
        N_EDGES = 100000
        X_DIM = 32
        E_DIM = 32
        HID = 64
        OUT = 32
        num_nodes = x.shape[0]
        rol, col = (edge_index[0], edge_index[1])
        e_feat = jnp.concatenate([x[rol], x[col], edge_attr], axis=-1)
        h = jax.nn.relu(e_feat @ W1 + b1)
        v = h @ W2 + b2
        x_cand = jax.ops.segment_max(v, col, num_segments=num_nodes)
        return jnp.maximum(x_cand, x[:, -v.shape[-1]:])
    edge_index = jnp.stack([src, dst])
    h = jnp.maximum(_layernorm(x, axis=-1), 0.0)
    x = x + _L0_gnn_ref(h, edge_index, edge_attr_32, L0_gnn_W1, L0_gnn_b1, L0_gnn_W2, L0_gnn_b2)
    return x

_drawn_inputs = setup_inputs


def setup_inputs(seed=0):
    import zlib

    import numpy as np

    out = dict(_drawn_inputs(seed))
    spreads = {'L0_gnn_b1': (0.0, 0.1), 'L0_gnn_b2': (0.0, 0.1)}
    factors = {}
    for name, (base, spread) in spreads.items():
        noise = np.random.default_rng([zlib.crc32(name.encode()), seed]).standard_normal(out[name].shape)
        drawn = base * np.exp(spread * noise) if base else spread * noise
        out[name] = jnp.asarray(drawn.astype(out[name].dtype))
    for name, factor in factors.items():
        out[name] = (out[name] * factor).astype(out[name].dtype)
    return out
```

```python
from contextlib import ExitStack

import concourse.bass as bass
from concourse import mybir

F32, BF16, I16, I32, U32 = mybir.dt.float32, mybir.dt.bfloat16, mybir.dt.int16, mybir.dt.int32, mybir.dt.uint32
ALU = mybir.AluOpType
ACT = mybir.ActivationFunctionType
AX_X = mybir.AxisListType.X

N, E, F, HID = 12500, 400000, 32, 64
EPS = 1e-5
P = 128
A = 4
R = 4
BLK = P * R
G = -(-E // (A * BLK))
while (E - G * BLK) % (A - 1):
    G += 1
LEN = G * BLK
S = (E - LEN) // (A - 1)
assert 0 < S <= LEN and (A - 1) * S + LEN == E

PN, NJ = 125, 100
assert PN * NJ == N
EP = E // PN
SEARCH = 640
BLOCKS = E // SEARCH
assert BLOCKS * SEARCH == E
HB = 5
NHB = NJ // HB

SLOTS = 4
PEEL = SLOTS + 1
assert (G - PEEL) % SLOTS == 0
TG = 32
NT = -(-G // TG)
ZCOL = 1000
ZDMAS = E * F // (P * ZCOL)
CLEARS_IN_FLIGHT, CLEARED_EARLY = 3, 4
assert ZDMAS * P * ZCOL == E * F
D = 16


def value_or_none(v):
    return None if isinstance(v, int) and v <= 0 else v


def wait(eng, sem, v):
    if value_or_none(v) is not None:
        eng.wait_ge(sem, v)


def over_groups(eng, step):
    for g in range(PEEL):
        step(g, g % SLOTS)
    with eng.Fori(0, (G - PEEL) // SLOTS) as i:
        for k in range(SLOTS):
            step(i * SLOTS + (PEEL + k), (PEEL + k) % SLOTS)


def build(nc, x, src, dst, edge_attr, W1, b1, W2, b2, out):
    ctx = ExitStack()
    with ctx:
        def sb(name, shape, dt=F32):
            return ctx.enter_context(nc.sbuf_tensor(name, shape, dt))

        def bank(name):
            return ctx.enter_context(nc.psum_tensor(name, [P, 512], F32))

        def sem(name):
            return ctx.enter_context(nc.semaphore(name))

        h_dram = nc.dram_tensor("h_dram", [N, F], F32, kind="Internal").ap()
        dst_dram = nc.dram_tensor("dst_dram", [BLOCKS, SEARCH], I16, kind="Internal").ap()
        same_dram = nc.dram_tensor("same_dram", [E], BF16, kind="Internal").ap()
        first_rows = nc.dram_tensor("first_rows", [E + N, F], F32, kind="Internal").ap()
        run_max = nc.dram_tensor("run_max", [A * LEN + 1, F], F32, kind="Internal").ap()

        x_sb = sb("x_sb", [PN, NJ, F])
        h_sb = sb("h_sb", [PN, NJ, F])
        work = sb("work", [PN, 2 * NJ * F])
        centred = work[:, 0:NJ * F].rearrange("p (j f) -> p j f", f=F)
        squared = work[:, NJ * F:2 * NJ * F].rearrange("p (j f) -> p j f", f=F)
        block_rows = work[:, 0:HB * SEARCH].bitcast(I16).rearrange("p (s k e) -> p s k e", s=2, k=HB)
        out_sb = work[:, 0:NJ * F].rearrange("p (j f) -> p j f", f=F)
        mean = sb("mean", [PN, NJ])
        var = sb("var", [PN, NJ])
        std = sb("std", [PN, NJ])
        rstd = sb("rstd", [PN, NJ])
        node_i = sb("node_i", [PN, NJ], I32)
        node = sb("node", [PN, NJ])
        below_node = sb("below_node", [PN, NJ])
        coarse = sb("coarse", [PN, NJ])
        fine = sb("fine", [PN, NJ])
        ended = sb("ended", [PN, NJ])
        block = sb("block", [PN, NJ])
        first = sb("first", [PN, NJ])
        nxt = sb("nxt", [PN, NJ])
        empty = sb("empty", [PN, NJ])
        tmp = sb("tmp", [PN, NJ])
        scatter_at = sb("scatter_at", [PN, NJ])
        last = sb("last", [PN, NJ])
        gather_at = sb("gather_at", [PN, NJ])
        junk = sb("junk", [PN, 2, SEARCH], I16)
        signs = sb("signs", [PN, 2, BLOCKS], BF16)
        ends_i = sb("ends_i", [1, BLOCKS], I32)
        ends_f = sb("ends_f", [1, BLOCKS])
        ends = sb("ends", [PN, BLOCKS])
        search_ix = sb("search_ix", [PN, 2 * HB], U32)
        scatter_ix = sb("scatter_ix", [PN, 2 * HB], U32)
        scatter_h = sb("scatter_h", [PN, 2, HB, F])
        gather_ix = sb("gather_ix", [PN, 2 * HB], U32)
        gathered_max = sb("gathered_max", [PN, 2, HB, F])
        carry_part = sb("carry_part", [PN, HB, F])
        start_ix = sb("start_ix", [A, 1], U32)
        start_rows = sb("start_rows", [A, F])
        start_i = sb("start_i", [PN, A - 1], I32)
        start_node = sb("start_node", [PN, A - 1])
        at_start = sb("at_start", [PN, A - 1, NJ])
        carry = sb("carry", [PN, A - 1, F])

        dst_i = sb("dst_i", [PN, EP], I32)
        dst_16 = sb("dst_16", [PN, EP], I16)
        before_i = sb("before_i", [PN, 1], I32)
        same = sb("same", [PN, EP], BF16)
        src_i = sb("src_i", [P, NT, BLK], I32)
        src_f = src_i[:, :, :].bitcast(F32)
        src_ix = sb("src_ix", [P, NT * TG, A, R], U32)

        ident = sb("ident", [P, P])
        ones = sb("ones", [1, PN])
        spread = sb("spread", [A, A, F], BF16)
        w1_blk = sb("w1_blk", [P, 3, 2, HID])
        w2_blk = sb("w2_blk", [P, 2, F])
        b1_col = sb("b1_col", [P, 1])
        b2_col = sb("b2_col", [P, 1])

        ea_in = sb("ea_in", [P, SLOTS, A, R * F])
        first_in = sb("first_in", [P, SLOTS, A, R * F])
        src_in = sb("src_in", [P, SLOTS, R, A, F])
        ea_at_r = sb("ea_at_r", [P, 2, R, A, F])
        first_at_r = sb("first_at_r", [P, 2, R, A, F])
        same_in = sb("same_in", [A, SLOTS, BLK], BF16)
        ix_ring = sb("ix_ring", [P, SLOTS, A * R], U32)
        same_t = sb("same_t", [P, 2, BLK])
        ea_t = sb("ea_t", [P, 2, BLK])
        src_t = sb("src_t", [P, 2, BLK])
        dst_t = sb("dst_t", [P, 2, BLK])
        hid = sb("hid", [P, 2, 2, BLK])
        zeros = hid[:, :, :, :].rearrange("p b q e -> p (b q e)")[:, 0:ZCOL]
        v_t = sb("v_t", [P, 2, BLK])
        max_t = sb("max_t", [P, 2, BLK])
        max_out = sb("max_out", [P, 2, A, R, F])

        ps_same, ps_ea, ps_src, ps_first = bank("ps_same"), bank("ps_ea"), bank("ps_src"), bank("ps_first")
        ps_hid = [bank("ps_hid0"), bank("ps_hid1")]
        ps_v, ps_back = bank("ps_v"), bank("ps_back")

        x_loaded, dst_loaded, ends_loaded, src_loaded = sem("x_loaded"), sem("dst_loaded"), sem("ends_loaded"), sem("src_loaded")
        weights_loaded, starts_loaded = sem("weights_loaded"), sem("starts_loaded")
        h_written, dst_written, same_written = sem("h_written"), sem("dst_written"), sem("same_written")
        rows_cleared = [sem(f"rows_cleared{c}") for c in range(CLEARS_IN_FLIGHT)]
        zero_row_written, start_rows_read, start_rows_written = sem("zero_row_written"), sem("start_rows_read"), sem("start_rows_written")
        next_shifted = sem("next_shifted")
        zeros_made, consts_made, idents_made, src_padded = sem("zeros_made"), sem("consts_made"), sem("idents_made"), sem("src_padded")
        ln_step, std_made, h_made = sem("ln_step"), sem("std_made"), sem("h_made")
        node_ready = sem("node_ready")
        dst_ready, same_made, ends_ready, ends_bcast, ends_copied = sem("dst_ready"), sem("same_made"), sem("ends_ready"), sem("ends_bcast"), sem("ends_copied")
        src_ready, src_turned, src_placed = sem("src_ready"), sem("src_turned"), sem("src_placed")
        block_made = sem("block_made")
        coarse_done, search_staged, fine_done = sem("coarse_done"), sem("search_staged"), sem("fine_done")
        blocks_read = [sem("blocks_read0"), sem("blocks_read1")]
        place_step, first_made = sem("place_step"), sem("first_made")
        scatter_staged = sem("scatter_staged")
        scattered = [sem("scattered0"), sem("scattered1")]
        ea_loaded = [sem(f"ea_loaded{s}") for s in range(SLOTS)]
        first_loaded = [sem(f"first_loaded{s}") for s in range(SLOTS)]
        same_loaded = [sem(f"same_loaded{s}") for s in range(SLOTS)]
        src_gathered = [sem(f"src_gathered{s}") for s in range(SLOTS)]
        ix_staged, gathers_begun = sem("ix_staged"), sem("gathers_begun")
        first_ordered, ea_ordered = sem("first_ordered"), sem("ea_ordered")
        same_spread, first_turned, ea_turned, srcs_turned = sem("same_spread"), sem("first_turned"), sem("ea_turned"), sem("srcs_turned")
        same_copied, ea_copied, src_copied, first_placed, dst_filled = sem("same_copied"), sem("ea_copied"), sem("src_copied"), sem("first_placed"), sem("dst_filled")
        hid_summed = [sem("hid_summed0"), sem("hid_summed1")]
        hid_made = [sem("hid_made0"), sem("hid_made1")]
        v_summed, v_copied, max_scanned, max_turned, max_copied = sem("v_summed"), sem("v_copied"), sem("max_scanned"), sem("max_turned"), sem("max_copied")
        max_stored = [sem("max_stored0"), sem("max_stored1")]
        carry_loaded, gather_staged, final_step, final_done, out_written = sem("carry_loaded"), sem("gather_staged"), sem("final_step"), sem("final_done"), sem("out_written")
        max_gathered = [sem("max_gathered0"), sem("max_gathered1")]

        def by_group(t):
            return bass.AP(t.tensor, 0, [[R * F, P], [S * F, A], [BLK * F, G], [1, R * F]])

        ea_view = by_group(edge_attr)
        first_view = by_group(first_rows)
        same_view = bass.AP(same_dram.tensor, 0, [[S, A], [BLK, G], [1, BLK]])
        max_view = run_max[0:A * LEN, :].rearrange("(a g p r) f -> p a g (r f)", a=A, g=G, p=P)
        dst_flat = dst.rearrange("(p e) -> p e", p=PN)

        block_ = ctx.enter_context(nc.Block())

        def all_cleared(eng):
            for c in range(CLEARS_IN_FLIGHT):
                eng.wait_ge(rows_cleared[c], D * len(range(c, ZDMAS, CLEARS_IN_FLIGHT)))

        def halves(eng, to, fr, sem_):
            cut = PN // 16 * 16
            for lo, hi in ((0, cut), (cut, PN)):
                eng.dma_start(to[lo:hi], fr[lo:hi]).then_inc(sem_, D)

        @block_.sync
        def _(sp):
            cleared = first_rows[0:E, :].rearrange("n f -> (n f)").rearrange("(z p c) -> z p c", p=P, c=ZCOL)

            def clear(z0, z1):
                for z in range(z0, z1):
                    wait(sp, rows_cleared[z % CLEARS_IN_FLIGHT], D * (z // CLEARS_IN_FLIGHT))
                    sp.dma_start(cleared[z], zeros[:, :]).then_inc(rows_cleared[z % CLEARS_IN_FLIGHT], D)

            halves(sp, x_sb, x.rearrange("(p j) f -> p j f", p=PN), x_loaded)
            sp.wait_ge(src_padded, 1)
            full = G // TG
            for a in range(A):
                sp.dma_start(src_i[a * TG:(a + 1) * TG, 0:full, :],
                             src[a * S:a * S + full * TG * BLK].rearrange("(t g e) -> g t e", g=TG, e=BLK)).then_inc(src_loaded, D)
                sp.dma_start(src_i[a * TG:a * TG + G - full * TG, full, :],
                             src[a * S + full * TG * BLK:a * S + LEN].rearrange("(g e) -> g e", e=BLK)).then_inc(src_loaded, D)
            sp.dma_start(ends_i[:, :], dst.rearrange("(o b e) -> o b e", o=1, e=SEARCH)[:, :, SEARCH - 1],
                         allow_slow_non_contiguous=True).then_inc(ends_loaded, D)
            halves(sp, dst_i, dst_flat, dst_loaded)
            sp.dma_start(before_i[1:PN, :], dst_flat[0:PN - 1, EP - 1:EP],
                         allow_slow_non_contiguous=True).then_inc(dst_loaded, D)
            sp.dma_start(start_ix[:, :], bass.AP(dst.tensor, 0, [[S, A], [1, 1]]).bitcast(U32),
                         allow_slow_non_contiguous=True).then_inc(starts_loaded, D)
            sp.dma_start(start_i[:, :], bass.AP(dst.tensor, S, [[0, PN], [S, A - 1]]),
                         allow_slow_non_contiguous=True).then_inc(starts_loaded, D)
            sp.wait_ge(zeros_made, 1)
            sp.wait_ge(consts_made, 4)
            for a in range(A):
                for part in range(3):
                    sp.dma_start(w1_blk[a * F:(a + 1) * F, part, a % 2, :], W1[part * F:(part + 1) * F, :]).then_inc(weights_loaded, D)
                sp.dma_start(b2_col[a * F:(a + 1) * F, :], b2.rearrange("(f o) -> f o", o=1)).then_inc(weights_loaded, D)
            for a in range(2):
                sp.dma_start(w2_blk[a * HID:(a + 1) * HID, a, :], W2).then_inc(weights_loaded, D)
                sp.dma_start(b1_col[a * HID:(a + 1) * HID, :], b1.rearrange("(f o) -> f o", o=1)).then_inc(weights_loaded, D)
            clear(0, CLEARED_EARLY)
            sp.wait_ge(h_made, 1)
            halves(sp, h_dram.rearrange("(p j) f -> p j f", p=PN), h_sb, h_written)
            sp.wait_ge(dst_ready, 1)
            halves(sp, dst_dram.rearrange("b e -> (b e)").rearrange("(p e) -> p e", p=PN), dst_16, dst_written)
            sp.wait_ge(same_made, 3)
            halves(sp, same_dram.rearrange("(p e) -> p e", p=PN), same, same_written)
            sp.dma_start(run_max[A * LEN:A * LEN + 1, :], zeros[0:1, 0:F]).then_inc(zero_row_written, D)
            clear(CLEARED_EARLY, ZDMAS)
            all_cleared(sp)
            sp.wait_ge(start_rows_read, D)
            sp.dma_start(bass.AP(first_rows.tensor, 0, [[S * F, A], [1, F]]), start_rows[:, :]).then_inc(start_rows_written, D)
            sp.wait_ge(first_made, 3)
            sp.dma_start(nxt[0:PN - 1, NJ - 1:NJ], first[1:PN, 0:1], allow_slow_non_contiguous=True).then_inc(next_shifted, D)
            sp.wait_ge(same_written, 2 * D)

            def store(g, par):
                sp.wait_ge(max_copied, g + 1)
                sp.dma_start(max_view[:, :, bass.ds(g, 1), :].rearrange("p a o e -> p (a o) e"),
                             max_out[:, par, :, :, :].rearrange("p a r f -> p a (r f)")).then_inc(max_stored[par], D)

            def step(g, slot):
                wait(sp, ea_ordered, g - SLOTS + 1)
                sp.dma_start(ea_in[:, slot, :, :], ea_view[:, :, bass.ds(g, 1), :].rearrange("p a o e -> p (a o) e")).then_inc(ea_loaded[slot], D)
                wait(sp, same_spread, g - SLOTS + 1)
                sp.dma_start(same_in[:, slot, :], same_view[:, bass.ds(g, 1), :].rearrange("a o e -> a (o e)")).then_inc(same_loaded[slot], D)
                if isinstance(g, int) and g == 0:
                    for s in scattered:
                        sp.wait_ge(s, D * HB * NHB // 2)
                wait(sp, first_ordered, g - SLOTS + 1)
                sp.dma_start(first_in[:, slot, :, :], first_view[:, :, bass.ds(g, 1), :].rearrange("p a o e -> p (a o) e")).then_inc(first_loaded[slot], D)
                if not isinstance(g, int) or g >= PEEL:
                    store(g - PEEL, (slot - PEEL) % 2)

            over_groups(sp, step)
            for g in range(G - PEEL, G):
                store(g, g % 2)
            for par in range(2):
                sp.wait_ge(max_stored[par], D * ((G + 1 - par) // 2))
            sp.dma_start(carry[:, :, :], bass.AP(run_max.tensor, S * F, [[0, PN], [LEN * F, A - 1], [1, F]])).then_inc(carry_loaded, D)
            with sp.Fori(0, NHB // 2) as i:
                sp.wait_ge(final_done, i * 2 + 2)
                cols = bass.ds(i * (2 * HB), 2 * HB)
                sp.dma_start(out.rearrange("(p j) f -> p j f", p=PN)[:, cols, :], out_sb[:, cols, :]).then_inc(out_written, D)
            sp.wait_ge(out_written, D * NHB // 2)

        @block_.gpsimd
        def _(pool):
            pool.memset(src_i[:, NT - 1, :], 0).then_inc(src_padded, 1)
            pool.memset(zeros[:, :], 0.0).then_inc(zeros_made, 1)
            pool.memset(ident[:, :], 0.0).then_inc(consts_made, 1)
            pool.memset(spread[:, :, :], 0.0).then_inc(consts_made, 1)
            pool.memset(w1_blk[:, :, :, :], 0.0).then_inc(consts_made, 1)
            pool.memset(w2_blk[:, :, :], 0.0).then_inc(consts_made, 1)
            pool.memset(ones[:, :], 1.0).then_inc(idents_made, 1)
            pool.iota(node_i[:, :], pattern=[[1, NJ]], base=0, channel_multiplier=NJ).then_inc(idents_made, 1)
            pool.wait_ge(consts_made, 4)
            pool.affine_select(out=ident[:, :], in_=ident[:, :], compare_op=ALU.not_equal, fill=1.0,
                               base=0, pattern=[[-1, P]], channel_multiplier=1).then_inc(idents_made, 1)
            pool.affine_select(out=spread[:, :, :], in_=spread[:, :, :], compare_op=ALU.not_equal, fill=1.0,
                               base=0, pattern=[[-1, A], [0, F]], channel_multiplier=1).then_inc(idents_made, 1)

            def gather_group(g, slot):
                pool.wait_ge(ix_staged, g + 1)
                wait(pool, srcs_turned, g - SLOTS + 1)
                pool.sem_inc(gathers_begun, 1)
                for a in range(A):
                    for r in range(R):
                        pool.indirect_dma_start(
                            out=src_in[:, slot, r, a, :], out_offset=None, in_=h_dram[:, :],
                            in_offset=bass.IndirectOffsetOnAxis(ap=ix_ring[:, slot, a * R + r:a * R + r + 1], axis=0),
                        ).then_inc(src_gathered[slot], D)

            pool.wait_ge(starts_loaded, 2 * D)
            pool.wait_ge(h_written, 2 * D)
            pool.indirect_dma_start(out=start_rows[:, :], out_offset=None, in_=h_dram[:, :],
                                    in_offset=bass.IndirectOffsetOnAxis(ap=start_ix[:, 0:1], axis=0)).then_inc(start_rows_read, D)
            for g in range(SLOTS - 1):
                gather_group(g, g)

            def read_blocks(hb, half):
                pool.wait_ge(search_staged, hb + 1)
                pool.sem_inc(gathers_begun, 1)
                for k in range(HB):
                    pool.indirect_dma_start(
                        out=block_rows[:, half, k, :], out_offset=None, in_=dst_dram[:, :],
                        in_offset=bass.IndirectOffsetOnAxis(ap=search_ix[:, half * HB + k:half * HB + k + 1], axis=0),
                    ).then_inc(blocks_read[half], D)

            pool.wait_ge(dst_written, 2 * D)
            for half in range(2):
                read_blocks(half, half)
            with pool.Fori(1, NHB // 2) as i:
                for half in range(2):
                    read_blocks(i * 2 + half, half)

            gather_group(SLOTS - 1, SLOTS - 1)

            pool.wait_ge(start_rows_written, D)
            all_cleared(pool)
            with pool.Fori(0, NHB // 2) as i:
                for half in range(2):
                    pool.wait_ge(scatter_staged, i * 2 + half + 1)
                    pool.sem_inc(gathers_begun, 1)
                    for k in range(HB):
                        pool.indirect_dma_start(
                            out=first_rows[:, :],
                            out_offset=bass.IndirectOffsetOnAxis(ap=scatter_ix[:, half * HB + k:half * HB + k + 1], axis=0),
                            in_=scatter_h[:, half, k, :], in_offset=None,
                        ).then_inc(scattered[half], D)

            gather_group(SLOTS, 0)
            with pool.Fori(0, (G - PEEL) // SLOTS) as i:
                for k in range(SLOTS):
                    gather_group(i * SLOTS + (PEEL + k), (PEEL + k) % SLOTS)

            for par in range(2):
                pool.wait_ge(max_stored[par], D * ((G + 1 - par) // 2))
            pool.wait_ge(zero_row_written, D)
            with pool.Fori(0, NHB // 2) as i:
                for half in range(2):
                    pool.wait_ge(gather_staged, i * 2 + half + 1)
                    pool.sem_inc(gathers_begun, 1)
                    for k in range(HB):
                        pool.indirect_dma_start(
                            out=gathered_max[:, half, k, :], out_offset=None, in_=run_max[:, :],
                            in_offset=bass.IndirectOffsetOnAxis(ap=gather_ix[:, half * HB + k:half * HB + k + 1], axis=0),
                        ).then_inc(max_gathered[half], D)

        @block_.scalar
        def _(act):
            act.wait_ge(src_loaded, 2 * A * D)
            for t in range(NT):
                nc.scalar.copy(src_f[:, t, :], src_i[:, t, :]).then_inc(src_ready, 1)

            def place_src(t):
                act.wait_ge(src_turned, t + 1)
                bk = (ps_same, ps_ea)[t % 2]
                nc.scalar.copy(src_ix[:, t * TG:(t + 1) * TG, :, :],
                               bk[:, :].rearrange("p (r a g) -> p g a r", r=R, a=A)).then_inc(src_placed, 1)

            def stage_ix(g, slot, gathered):
                if gathered is not None:
                    act.wait_ge(src_gathered[slot], gathered)
                nc.scalar.copy(ix_ring[:, slot, :],
                               src_ix[:, bass.ds(g, 1), :, :].rearrange("p o a r -> p (o a r)")).then_inc(ix_staged, 1)

            place_src(0)
            act.wait_ge(src_placed, 1)
            for g in range(SLOTS):
                stage_ix(g, g, None)
            act.wait_ge(ends_bcast, 1)
            nc.scalar.copy(ends[:, 0:500], ps_src[0:PN, 0:500]).then_inc(ends_copied, 1)
            nc.scalar.copy(ends[:, 500:BLOCKS], ps_first[0:PN, 0:BLOCKS - 500]).then_inc(ends_copied, 1)
            act.wait_ge(dst_loaded, 3 * D)
            nc.scalar.copy(dst_16[:, :], dst_i[:, :]).then_inc(dst_ready, 1)
            act.wait_ge(ln_step, 7)
            nc.scalar.activation(std[:, :], var[:, :], ACT.Sqrt).then_inc(std_made, 1)
            for t in range(1, NT):
                place_src(t)

            def count_blocks(j, buf):
                wait(act, coarse_done, j - 1)
                nc.scalar.activation(signs[:, buf, :], ends[:, :], ACT.Sign, bias=below_node[:, bass.ds(j, 1)], scale=-1.0,
                                     accum_out=coarse[:, bass.ds(j, 1)]).then_inc(coarse_done, 1)

            act.wait_ge(node_ready, 2)
            act.wait_ge(ends_copied, 2)
            count_blocks(0, 0)
            count_blocks(1, 1)
            with act.Fori(1, NJ // 2) as i:
                for buf in range(2):
                    count_blocks(i * 2 + buf, buf)
            act.wait_ge(src_placed, NT)
            act.wait_ge(weights_loaded, D * (4 * A + 4))

            def finish(g, par):
                act.wait_ge(v_summed, g + 1)
                wait(act, max_scanned, g - 1)
                nc.scalar.activation(v_t[:, par, :], ps_v[:, :], ACT.Identity, bias=b2_col[:, 0:1]).then_inc(v_copied, 1)

            def order_rows(g, slot, landed):
                for tile, loaded, ordered, turned, done in ((first_in, first_loaded, first_at_r, first_turned, first_ordered),
                                                            (ea_in, ea_loaded, ea_at_r, ea_turned, ea_ordered)):
                    act.wait_ge(loaded[slot], landed)
                    wait(act, turned, g - 1)
                    nc.scalar.copy(ordered[:, slot % 2, :, :, :],
                                   tile[:, slot, :, :].rearrange("p a (r f) -> p r a f", r=R)).then_inc(done, 1)

            def step(g, slot, stored, landed):
                par = slot % 2
                order_rows(g, slot, landed)
                act.wait_ge(same_spread, g + 1)
                wait(act, max_scanned, g - 1)
                nc.scalar.copy(same_t[:, par, :], ps_same[:, :]).then_inc(same_copied, 1)
                act.wait_ge(ea_turned, g + 1)
                wait(act, hid_summed[1], g - 1)
                nc.scalar.copy(ea_t[:, par, :].rearrange("p (q r) -> p q r", r=R),
                               ps_ea[:, :].rearrange("p (r q) -> p q r", r=R)).then_inc(ea_copied, 1)
                if not isinstance(g, int) or g >= 1:
                    finish(g - 1, 1 - par)
                act.wait_ge(hid_summed[0], g + 1)
                wait(act, v_summed, g - 1)
                nc.scalar.activation(hid[:, par, 0, :], ps_hid[0][:, :], ACT.Relu, bias=b1_col[:, 0:1]).then_inc(hid_made[0], 1)
                if not isinstance(g, int) or g >= 1:
                    hand_out(g - 1, 1 - par, stored)

            def hand_out(g, par, stored):
                act.wait_ge(max_turned, g + 1)
                wait(act, max_stored[par], stored)
                nc.scalar.copy(max_out[:, par, :, :, :],
                               ps_back[:, :].rearrange("p (r a f) -> p a r f", r=R, a=A)).then_inc(max_copied, 1)

            for g in range(PEEL):
                step(g, g % SLOTS, D * ((g - 1) // 2), D * (g // SLOTS + 1))
                stage_ix(g + SLOTS, g % SLOTS, A * R * D * (g // SLOTS + 1))
            with act.Fori(0, (G - PEEL) // SLOTS) as i:
                for k in range(SLOTS):
                    g = i * SLOTS + (PEEL + k)
                    slot = (PEEL + k) % SLOTS
                    step(g, slot, i * (D * SLOTS // 2) + D * ((PEEL + k - 1) // 2),
                         i * D + D * ((PEEL + k) // SLOTS + 1))
                    stage_ix(g + SLOTS, slot, i * (A * R * D) + A * R * D * ((PEEL + k) // SLOTS + 1))
            finish(G - 1, (G - 1) % 2)
            hand_out(G - 1, (G - 1) % 2, D * ((G - 1) // 2))

        @block_.tensor
        def _(pe):
            def spread_ends():
                pe.wait_ge(ends_ready, 1)
                nc.tensor.matmul(ps_src[0:PN, 0:500], ones[0:1, :], ends_f[0:1, 0:500], start=True, stop=True)
                nc.tensor.matmul(ps_first[0:PN, 0:BLOCKS - 500], ones[0:1, :], ends_f[0:1, 500:BLOCKS],
                                 start=True, stop=True).then_inc(ends_bcast, 1)

            pe.wait_ge(idents_made, 4)
            for t in range(NT):
                pe.wait_ge(src_ready, t + 1)
                wait(pe, src_placed, t - 1)
                bk = (ps_same, ps_ea)[t % 2]
                for r in range(R):
                    mm = nc.tensor.transpose(bk[:, r * P:(r + 1) * P], src_f[:, t, r:BLK:R], ident[:, :])
                mm.then_inc(src_turned, 1)
                if t == 1:
                    spread_ends()
            pe.wait_ge(ends_copied, 2)
            pe.wait_ge(src_placed, NT)
            pe.wait_ge(weights_loaded, D * (4 * A + 4))

            def turn(bk, tile, buf):
                for r in range(R):
                    mm = nc.tensor.transpose(bk[:, r * P:(r + 1) * P],
                                             tile[:, buf, r, :, :].rearrange("p a f -> p (a f)"), ident[:, :])
                return mm

            def inputs(g, slot, landed):
                pe.wait_ge(same_loaded[slot], landed(D))
                wait(pe, same_copied, g)
                nc.tensor.matmul(ps_same[:, :], spread[:, :, :].rearrange("k a f -> k (a f)"), same_in[:, slot, :],
                                 start=True, stop=True).then_inc(same_spread, 1)
                pe.wait_ge(ea_ordered, g + 1)
                wait(pe, ea_copied, g)
                turn(ps_ea, ea_at_r, slot % 2).then_inc(ea_turned, 1)
                pe.wait_ge(src_gathered[slot], landed(D * A * R))
                wait(pe, src_copied, g)
                turn(ps_src, src_in, slot).then_inc(srcs_turned, 1)
                pe.wait_ge(first_ordered, g + 1)
                wait(pe, dst_filled, g)
                turn(ps_first, first_at_r, slot % 2).then_inc(first_turned, 1)

            def layer_one(g, par):
                for q in range(2):
                    wait(pe, hid_made[q], g)
                    rows = slice(q * 2 * F, (q + 1) * 2 * F)
                    for n, (part, t, ready) in enumerate(((2, ea_t, ea_copied), (0, src_t, src_copied), (1, dst_t, dst_filled))):
                        pe.wait_ge(ready, g + 1)
                        mm = nc.tensor.matmul(ps_hid[q][:, :], w1_blk[rows, part, :, :].rearrange("k a h -> k (a h)"),
                                              t[rows, par, :], start=(n == 0), stop=(n == 2))
                    mm.then_inc(hid_summed[q], 1)

            def layer_two(g, par):
                wait(pe, v_copied, g)
                for q in range(2):
                    pe.wait_ge(hid_made[q], g + 1)
                    mm = nc.tensor.matmul(ps_v[q * 2 * F:(q + 1) * 2 * F, :], w2_blk[:, :, :].rearrange("k a f -> k (a f)"),
                                          hid[:, par, q, :], start=True, stop=True)
                mm.then_inc(v_summed, 1)

            def turn_back(g, par):
                pe.wait_ge(max_scanned, g + 1)
                wait(pe, max_copied, g)
                for r in range(R):
                    mm = nc.tensor.transpose(ps_back[:, r * P:(r + 1) * P], max_t[:, par, r:BLK:R], ident[:, :])
                mm.then_inc(max_turned, 1)

            def step(g, slot, landed):
                par = slot % 2
                inputs(g, slot, landed)
                if not isinstance(g, int) or g >= 1:
                    layer_two(g - 1, 1 - par)
                layer_one(g, par)
                if not isinstance(g, int) or g >= 1:
                    turn_back(g - 1, 1 - par)

            for g in range(PEEL):
                step(g, g % SLOTS, lambda unit: unit * (g // SLOTS + 1))
            with pe.Fori(0, (G - PEEL) // SLOTS) as i:
                for k in range(SLOTS):
                    step(i * SLOTS + (PEEL + k), (PEEL + k) % SLOTS,
                         lambda unit: i * unit + unit * ((PEEL + k) // SLOTS + 1))
            layer_two(G - 1, (G - 1) % 2)
            turn_back(G - 1, (G - 1) % 2)

        @block_.vector
        def _(dve):
            V = nc.vector
            dve.wait_ge(ends_loaded, D)
            V.tensor_copy(ends_f[:, :], ends_i[:, :]).then_inc(ends_ready, 1)
            dve.wait_ge(x_loaded, 2 * D)
            V.tensor_reduce(mean[:, :], x_sb[:, :, :], AX_X, ALU.add).then_inc(ln_step, 1)
            dve.wait_ge(ln_step, 1)
            V.tensor_scalar(mean[:, :], mean[:, :], 1.0 / F, None, ALU.mult).then_inc(ln_step, 1)
            dve.wait_ge(ln_step, 2)
            V.tensor_tensor(centred, x_sb[:, :, :], mean[:, :].unsqueeze(2).broadcast_to([PN, NJ, F]), ALU.subtract).then_inc(ln_step, 1)
            dve.wait_ge(ln_step, 3)
            V.tensor_tensor(squared, centred, centred, ALU.mult).then_inc(ln_step, 1)
            dve.wait_ge(ln_step, 4)
            V.tensor_reduce(var[:, :], squared, AX_X, ALU.add).then_inc(ln_step, 1)
            dve.wait_ge(ln_step, 5)
            V.tensor_scalar(var[:, :], var[:, :], 1.0 / F, EPS, ALU.mult, ALU.add).then_inc(ln_step, 2)
            dve.wait_ge(std_made, 1)
            V.reciprocal(rstd[:, :], std[:, :]).then_inc(ln_step, 1)
            dve.wait_ge(ln_step, 8)
            V.scalar_tensor_tensor(out=h_sb[:, :, :], in0=centred, scalar=0.0,
                                   in1=rstd[:, :].unsqueeze(2).broadcast_to([PN, NJ, F]),
                                   op0=ALU.max, op1=ALU.mult).then_inc(h_made, 1)
            dve.wait_ge(idents_made, 4)
            V.tensor_copy(node[:, :], node_i[:, :]).then_inc(node_ready, 1)
            dve.wait_ge(node_ready, 1)
            V.tensor_scalar(below_node[:, :], node[:, :], -0.5, None, ALU.add).then_inc(node_ready, 1)
            dve.wait_ge(dst_loaded, 3 * D)
            V.memset(before_i[0:1, :], -1).then_inc(same_made, 1)
            V.tensor_tensor(same[:, 1:EP], dst_i[:, 1:EP], dst_i[:, 0:EP - 1], ALU.is_equal).then_inc(same_made, 1)
            dve.wait_ge(same_made, 1)
            V.tensor_tensor(same[:, 0:1], dst_i[:, 0:1], before_i[:, :], ALU.is_equal).then_inc(same_made, 1)

            def stage_search(hb, half):
                cols = bass.ds(hb * HB, HB)
                dve.wait_ge(coarse_done, hb * HB + HB)
                V.tensor_scalar(ended[:, cols], coarse[:, cols], 0.5, BLOCKS / 2, ALU.mult, ALU.add).then_inc(block_made, 1)
                dve.wait_ge(block_made, hb + 1)
                V.tensor_scalar(search_ix[:, half * HB:(half + 1) * HB], ended[:, cols], float(BLOCKS - 1), None, ALU.min).then_inc(search_staged, 1)

            def count_below(hb, half, landed):
                dve.wait_ge(blocks_read[half], landed)
                for k in range(HB):
                    col = bass.ds(hb * HB + k, 1)
                    if k >= 2:
                        dve.wait_ge(fine_done, hb * HB + (k - 1))
                    V.tensor_scalar(junk[:, k % 2, :], block_rows[:, half, k, :], node[:, col], None, ALU.is_lt, ALU.add,
                                    accum_out=fine[:, col]).then_inc(fine_done, 1)
                dve.wait_ge(fine_done, hb * HB + HB)

            stage_search(0, 0)
            stage_search(1, 1)
            with dve.Fori(0, NHB // 2 - 1) as i:
                for half in range(2):
                    count_below(i * 2 + half, half, i * (D * HB) + D * HB)
                    stage_search(i * 2 + (half + 2), half)
            for half in range(2):
                count_below(NHB - 2 + half, half, D * HB * NHB // 2)

            V.tensor_scalar(block[:, :], ended[:, :], float(BLOCKS - 1), None, ALU.min).then_inc(block_made, 1)
            dve.wait_ge(block_made, NHB + 1)

            V.scalar_tensor_tensor(out=first[:, :], in0=block[:, :], scalar=float(SEARCH), in1=fine[:, :],
                                   op0=ALU.mult, op1=ALU.add).then_inc(first_made, 1)
            V.memset(nxt[:, NJ - 1:NJ], float(E)).then_inc(first_made, 1)
            dve.wait_ge(first_made, 2)
            V.tensor_copy(nxt[:, 0:NJ - 1], first[:, 1:NJ]).then_inc(first_made, 1)
            dve.wait_ge(first_made, 3)
            dve.wait_ge(next_shifted, D)
            V.tensor_tensor(empty[:, :], first[:, :], nxt[:, :], ALU.is_equal).then_inc(place_step, 1)
            V.scalar_tensor_tensor(out=tmp[:, :], in0=node[:, :], scalar=float(E), in1=first[:, :],
                                   op0=ALU.add, op1=ALU.subtract).then_inc(place_step, 1)
            dve.wait_ge(place_step, 2)
            V.tensor_tensor(tmp[:, :], tmp[:, :], empty[:, :], ALU.mult).then_inc(place_step, 1)
            dve.wait_ge(place_step, 3)
            V.tensor_tensor(scatter_at[:, :], tmp[:, :], first[:, :], ALU.add).then_inc(place_step, 1)
            dve.wait_ge(place_step, 4)

            def stage_scatter(hb, half, landed):
                if landed is not None:
                    dve.wait_ge(scattered[half], landed)
                V.tensor_copy(scatter_ix[:, half * HB:(half + 1) * HB], scatter_at[:, bass.ds(hb * HB, HB)]).then_inc(place_step, 1)
                V.tensor_copy(scatter_h[:, half, :, :], h_sb[:, bass.ds(hb * HB, HB), :]).then_inc(scatter_staged, 1)

            stage_scatter(0, 0, None)
            stage_scatter(1, 1, None)
            with dve.Fori(1, NHB // 2) as i:
                for half in range(2):
                    stage_scatter(i * 2 + half, half, i * (D * HB))

            base = 4 + NHB
            dve.wait_ge(place_step, base)
            V.tensor_scalar(last[:, :], nxt[:, :], -1.0, None, ALU.add).then_inc(place_step, 1)
            dve.wait_ge(place_step, base + 1)
            V.tensor_copy(gather_at[:, :], last[:, :]).then_inc(place_step, 1)
            dve.wait_ge(place_step, base + 2)
            for a in range(1, A):
                V.tensor_scalar(tmp[:, :], last[:, :], float(a * S), float(LEN - S), ALU.is_ge, ALU.mult).then_inc(place_step, 1)
                dve.wait_ge(place_step, base + 1 + 2 * a)
                V.tensor_tensor(gather_at[:, :], gather_at[:, :], tmp[:, :], ALU.add).then_inc(place_step, 1)
                dve.wait_ge(place_step, base + 2 + 2 * a)
            base += 2 * A
            V.tensor_scalar(tmp[:, :], gather_at[:, :], -1.0, float(A * LEN), ALU.mult, ALU.add).then_inc(place_step, 1)
            dve.wait_ge(place_step, base + 1)
            V.tensor_tensor(tmp[:, :], tmp[:, :], empty[:, :], ALU.mult).then_inc(place_step, 1)
            dve.wait_ge(place_step, base + 2)
            V.tensor_tensor(gather_at[:, :], gather_at[:, :], tmp[:, :], ALU.add).then_inc(place_step, 1)
            dve.wait_ge(starts_loaded, 2 * D)
            V.tensor_copy(start_node[:, :], start_i[:, :]).then_inc(place_step, 1)
            dve.wait_ge(place_step, base + 4)
            for a in range(A - 1):
                V.tensor_scalar(at_start[:, a, :], node[:, :], start_node[:, a:a + 1], None, ALU.is_equal).then_inc(place_step, 1)
            base += 4 + A - 1
            dve.wait_ge(place_step, base)

            def scan_max(g, par):
                dve.wait_ge(v_copied, g + 1)
                dve.wait_ge(same_copied, g + 1)
                wait(dve, max_turned, g - 1)
                wait(dve, max_scanned, g)
                V.tensor_tensor_scan(max_t[:, par, :], same_t[:, par, :], v_t[:, par, :],
                                     0.0 if isinstance(g, int) and g == 0 else max_t[:, 1 - par, BLK - 1:BLK],
                                     ALU.mult, ALU.max).then_inc(max_scanned, 1)

            def by_edge(bk):
                return bk[:, :].rearrange("p (r q) -> p q r", r=R)

            def step(g, slot):
                par = slot % 2
                wait(dve, hid_summed[1], g - 1)
                dve.wait_ge(srcs_turned, g + 1)
                V.tensor_copy(src_t[:, par, :].rearrange("p (q r) -> p q r", r=R), by_edge(ps_src)).then_inc(src_copied, 1)
                dve.wait_ge(first_turned, g + 1)
                wait(dve, hid_summed[1], g - 1)
                V.tensor_copy(dst_t[:, par, :].rearrange("p (q r) -> p q r", r=R), by_edge(ps_first)).then_inc(first_placed, 1)
                dve.wait_ge(first_placed, g + 1)
                dve.wait_ge(same_copied, g + 1)
                wait(dve, dst_filled, g)
                V.tensor_tensor_scan(dst_t[:, par, :], same_t[:, par, :], dst_t[:, par, :],
                                     0.0 if isinstance(g, int) and g == 0 else dst_t[:, 1 - par, BLK - 1:BLK],
                                     ALU.mult, ALU.max).then_inc(dst_filled, 1)
                if not isinstance(g, int) or g >= 1:
                    scan_max(g - 1, 1 - par)
                dve.wait_ge(hid_summed[1], g + 1)
                wait(dve, v_summed, g - 1)
                V.tensor_scalar(hid[:, par, 1, :], ps_hid[1][:, :], b1_col[:, 0:1], 0.0, ALU.add, ALU.max).then_inc(hid_made[1], 1)

            dve.wait_ge(weights_loaded, D * (4 * A + 4))
            over_groups(dve, step)
            scan_max(G - 1, (G - 1) % 2)

            def stage_gather(hb, half):
                V.tensor_copy(gather_ix[:, half * HB:(half + 1) * HB], gather_at[:, bass.ds(hb * HB, HB)]).then_inc(gather_staged, 1)

            STEPS = 2 * A

            def finish(hb, half, landed):
                cols = bass.ds(hb * HB, HB)
                got = gathered_max[:, half, :, :]
                dve.wait_ge(max_gathered[half], landed)
                n = 0
                for a in range(A - 1):
                    V.tensor_tensor(carry_part[:, :, :], at_start[:, a, cols].unsqueeze(2).broadcast_to([PN, HB, F]),
                                    carry[:, a, :].unsqueeze(1).broadcast_to([PN, HB, F]), ALU.mult).then_inc(final_step, 1)
                    n += 1
                    dve.wait_ge(final_step, hb * (STEPS - 1) + n)
                    V.tensor_tensor(got, got, carry_part[:, :, :], ALU.max).then_inc(final_step, 1)
                    n += 1
                    dve.wait_ge(final_step, hb * (STEPS - 1) + n)
                V.tensor_tensor(got, got, h_sb[:, cols, :], ALU.max).then_inc(final_step, 1)
                n += 1
                dve.wait_ge(final_step, hb * (STEPS - 1) + n)
                V.tensor_tensor(out_sb[:, cols, :], got, x_sb[:, cols, :], ALU.add).then_inc(final_done, 1)
                dve.wait_ge(final_done, hb + 1)

            stage_gather(0, 0)
            stage_gather(1, 1)
            dve.wait_ge(carry_loaded, D)
            with dve.Fori(0, NHB // 2 - 1) as i:
                for half in range(2):
                    finish(i * 2 + half, half, i * (D * HB) + D * HB)
                    stage_gather(i * 2 + (half + 2), half)
            for half in range(2):
                finish(NHB - 2 + half, half, D * HB * NHB // 2)


_INS = ['x', 'src', 'dst', 'edge_attr_32', 'L0_gnn_W1', 'L0_gnn_b1', 'L0_gnn_W2', 'L0_gnn_b2']
_OUTS = [((N, F), 'float32')]


def kernel(**inputs):
    import numpy as _np
    import concourse.bacc as _bacc
    from concourse import mybir as _mybir
    from concourse.bass_utils import run_bass_kernel_spmd as _run

    nc = _bacc.Bacc("TRN2", target_bir_lowering=False, num_devices=1)
    arrays, args = {}, []
    for name in _INS:
        a = _np.ascontiguousarray(inputs[name])
        arrays[f"in_{name}_dram"] = a
        args.append(nc.dram_tensor(f"in_{name}_dram", a.shape, _mybir.dt.from_np(a.dtype), kind="ExternalInput").ap())
    for i, (shape, dtype) in enumerate(_OUTS):
        dt = _mybir.dt.from_np(_np.dtype(dtype))
        args.append(nc.dram_tensor(f"out_{i}_dram", shape, dt, kind="ExternalOutput").ap())
    build(nc, *args)
    r = _run(nc, [arrays], core_ids=[0])
    got = tuple(r.results[0][f"out_{i}_dram"] for i in range(len(_OUTS)))
    return got[0]
```

```python
from contextlib import ExitStack

import concourse.bass as bass
from concourse import mybir

F32, BF16, I16, I32, U32 = mybir.dt.float32, mybir.dt.bfloat16, mybir.dt.int16, mybir.dt.int32, mybir.dt.uint32
ALU = mybir.AluOpType
ACT = mybir.ActivationFunctionType
AX_X = mybir.AxisListType.X

N, E, F, HID = 12500, 400000, 32, 64
EPS = 1e-5
P = 128
A = 4
LANES = P // A
R = 16
BLK = LANES * R
assert LANES == F == 32
G = -(-E // (A * BLK))
while (E - G * BLK) % (A - 1):
    G += 1
LEN = G * BLK
S = (E - LEN) // (A - 1)
assert 0 < S <= LEN and (A - 1) * S + LEN == E

PN, NJ = 125, 100
assert PN * NJ == N
EP = E // PN
SEARCH = 640
BLOCKS = E // SEARCH
assert BLOCKS * SEARCH == E
HB = 5
NHB = NJ // HB

SLOTS = 4
PAIRS = (G - 1) // 2
assert G % 2 == 1 and PAIRS % 2 == 0
PICK = R - 1
PARTS = 3
TILES = -(-N // P)
CT = 7
CHUNKS = TILES // CT
assert CHUNKS * CT == TILES
RING = 2
assert CHUNKS % RING == 0
PLACES = ((2, 1, 1), (2, 1, 1), (2, 1, 0), (2, 1, 0))
assert sum(map(sum, PLACES)) == CHUNKS
PAD = 2 * SLOTS * BLK
ZCOL = 1000
ZDMAS = E * F // (P * ZCOL)
CLEARS_IN_FLIGHT, CLEARED_EARLY = 3, 4
assert ZDMAS * P * ZCOL == E * F
D = 16


def value_or_none(v):
    return None if isinstance(v, int) and v <= 0 else v


def wait(eng, sem, v):
    if value_or_none(v) is not None:
        eng.wait_ge(sem, v)


def over_pairs(eng, first_group, pair):
    first_group()
    for half in range(2):
        pair(half, half, 1)
    with eng.Fori(0, PAIRS // 2 - 1) as i:
        for half in range(2):
            pair(i * 2 + (half + 2), half, i + 2)


def over_groups(eng, step):
    def pair(j, half, turn):
        for m in range(2):
            step(j * 2 + (m + 1), half * 2 + m, turn)

    over_pairs(eng, lambda: step(0, SLOTS - 1, 0), pair)


def is_first(turn):
    return isinstance(turn, int) and turn == 0


def gathers_by(slot, turn):
    full = slot == SLOTS - 1
    if isinstance(turn, int) and turn <= 1:
        return (turn + full) * (R * D)
    return turn * ((R - 1) * D) + (D + full * R * D)


def chunk_at(slot, place, m):
    return sum(map(sum, PLACES[:slot])) + sum(PLACES[slot][:place]) + m


def build(nc, x, src, dst, edge_attr, W1, b1, W2, b2, out):
    ctx = ExitStack()
    with ctx:
        def sb(name, shape, dt=F32):
            return ctx.enter_context(nc.sbuf_tensor(name, shape, dt))

        def bank(name):
            return ctx.enter_context(nc.psum_tensor(name, [P, 512], F32))

        def sem(name):
            return ctx.enter_context(nc.semaphore(name))

        src_pad = nc.dram_tensor("src_pad", [E + PAD], I32, kind="Internal").ap()
        h_dram = nc.dram_tensor("h_dram", [N, F], F32, kind="Internal").ap()
        dst_dram = nc.dram_tensor("dst_dram", [BLOCKS, SEARCH], I16, kind="Internal").ap()
        same_dram = nc.dram_tensor("same_dram", [E], BF16, kind="Internal").ap()
        first_rows = nc.dram_tensor("first_rows", [E + N, F], F32, kind="Internal").ap()
        run_max = nc.dram_tensor("run_max", [A * LEN + 1, F], F32, kind="Internal").ap()

        x_sb = sb("x_sb", [PN, NJ, F])
        h_sb = sb("h_sb", [PN, NJ, F])
        work_all = sb("work", [P, 2 * NJ * F])
        work = work_all[0:PN, :]
        table_f = work_all[:, NJ * F:NJ * F + TILES * F].rearrange("p (t f) -> p t f", f=F)
        centred = work[:, 0:NJ * F].rearrange("p (j f) -> p j f", f=F)
        squared = work[:, NJ * F:2 * NJ * F].rearrange("p (j f) -> p j f", f=F)
        block_rows = work[:, 0:HB * SEARCH].bitcast(I16).rearrange("p (s k e) -> p s k e", s=2, k=HB)
        out_sb = work[:, 0:NJ * F].rearrange("p (j f) -> p j f", f=F)
        mean = sb("mean", [PN, NJ])
        var = sb("var", [PN, NJ])
        std = sb("std", [PN, NJ])
        rstd = sb("rstd", [PN, NJ])
        node_i = sb("node_i", [PN, NJ], I32)
        node = sb("node", [PN, NJ])
        below_node = sb("below_node", [PN, NJ])
        coarse = sb("coarse", [PN, NJ])
        fine = sb("fine", [PN, NJ])
        ended = sb("ended", [PN, NJ])
        block = sb("block", [PN, NJ])
        first = sb("first", [PN, NJ])
        nxt = sb("nxt", [PN, NJ])
        empty = sb("empty", [PN, NJ])
        tmp = sb("tmp", [PN, NJ])
        scatter_at = sb("scatter_at", [PN, NJ])
        last = sb("last", [PN, NJ])
        gather_at = sb("gather_at", [PN, NJ])
        junk = sb("junk", [PN, 2, SEARCH], I16)
        signs = sb("signs", [PN, 2, BLOCKS], BF16)
        ends_i = sb("ends_i", [1, BLOCKS], I32)
        ends_f = sb("ends_f", [1, BLOCKS])
        ends = sb("ends", [PN, BLOCKS])
        search_ix = sb("search_ix", [PN, 2 * HB], U32)
        scatter_ix = sb("scatter_ix", [PN, 2 * HB], U32)
        scatter_h = sb("scatter_h", [PN, 2, HB, F])
        gather_ix = sb("gather_ix", [PN, 2 * HB], U32)
        gathered_max = sb("gathered_max", [PN, 2, HB, F])
        carry_part = sb("carry_part", [PN, HB, F])
        start_ix = sb("start_ix", [A, 1], U32)
        start_rows = sb("start_rows", [A, F])
        start_i = sb("start_i", [PN, A - 1], I32)
        start_node = sb("start_node", [PN, A - 1])
        at_start = sb("at_start", [PN, A - 1, NJ])
        carry = sb("carry", [PN, A - 1, F])

        dst_i = sb("dst_i", [PN, EP], I32)
        dst_16 = sb("dst_16", [PN, EP], I16)
        before_i = sb("before_i", [PN, 1], I32)
        same = sb("same", [PN, EP], BF16)

        table = sb("table", [P, TILES, PARTS * F], BF16)
        tile_node_i = sb("tile_node_i", [P, TILES], I32)
        tile_node = sb("tile_node", [P, TILES])
        ident = sb("ident", [P, P])
        add_parts = sb("add_parts", [PARTS * F, F])
        pick_i = sb("pick_i", [P, SLOTS], I32)
        pick_f = sb("pick_f", [P, SLOTS])
        pick_all = sb("pick_all", [P, SLOTS * P], I16)
        onehot = sb("onehot", [P, RING, CT, SLOTS * P], BF16)
        picked_parts = sb("picked_parts", [PARTS * F, SLOTS * P])

        ones = sb("ones", [1, PN])
        spread = sb("spread", [A, A, F], BF16)
        w1_blk = sb("w1_blk", [P, 3, 2, HID])
        w2_blk = sb("w2_blk", [P, 2, F])
        b1_col = sb("b1_col", [P, 1])
        b2_col = sb("b2_col", [P, 1])

        ea_in = sb("ea_in", [P, SLOTS, R, F])
        first_in = sb("first_in", [P, SLOTS, R, F])
        src_in = sb("src_in", [P, SLOTS, R, F])
        same_in = sb("same_in", [A, SLOTS, BLK], BF16)
        src_ix = sb("src_ix", [P, SLOTS, R], U32)
        ea_t = sb("ea_t", [P, 2, BLK])
        src_t = sb("src_t", [P, 2, BLK])
        dst_t = sb("dst_t", [P, 2, BLK])
        hid = sb("hid", [P, 2, 2, BLK])
        zeros = hid[:, :, :, :].rearrange("p b q e -> p (b q e)")[:, 0:ZCOL]
        v_t = sb("v_t", [P, 2, BLK])
        max_t = sb("max_t", [P, 2, BLK])
        max_out = sb("max_out", [P, SLOTS, R, F])

        ps_same = [bank("ps_same0"), bank("ps_same1")]
        ps_hid = [bank("ps_hid0"), bank("ps_hid1")]
        ps_v = bank("ps_v")
        ps_all, ps_parts, ps_pick = bank("ps_all"), bank("ps_parts"), bank("ps_pick")
        ps_ends = [ps_parts, ps_pick]

        x_loaded, dst_loaded, ends_loaded = sem("x_loaded"), sem("dst_loaded"), sem("ends_loaded")
        weights_loaded, starts_loaded = sem("weights_loaded"), sem("starts_loaded")
        h_written, dst_written, same_written = sem("h_written"), sem("dst_written"), sem("same_written")
        rows_cleared = [sem(f"rows_cleared{c}") for c in range(CLEARS_IN_FLIGHT)]
        zero_row_written, start_rows_read, start_rows_written = sem("zero_row_written"), sem("start_rows_read"), sem("start_rows_written")
        next_shifted = sem("next_shifted")
        zeros_made, consts_made, numbers_made = sem("zeros_made"), sem("consts_made"), sem("numbers_made")
        ln_step, std_made, h_made = sem("ln_step"), sem("std_made"), sem("h_made")
        node_ready = sem("node_ready")
        dst_ready, same_made, ends_ready, ends_bcast, ends_copied = sem("dst_ready"), sem("same_made"), sem("ends_ready"), sem("ends_bcast"), sem("ends_copied")
        block_made = sem("block_made")
        coarse_done, search_staged, fine_done = sem("coarse_done"), sem("search_staged"), sem("fine_done")
        blocks_read = [sem("blocks_read0"), sem("blocks_read1")]
        place_step, first_made = sem("place_step"), sem("first_made")
        scatter_staged = sem("scatter_staged")
        scattered = [sem("scattered0"), sem("scattered1")]
        ea_loaded = [sem(f"ea_loaded{s}") for s in ("0", "1", "_first")]
        first_loaded = [sem(f"first_loaded{s}") for s in ("0", "1", "_first")]
        same_loaded = [sem(f"same_loaded{s}") for s in ("0", "1", "_first")]
        ix_loaded = [sem(f"ix_loaded{s}") for s in ("0", "1", "_first")]
        max_stored = [sem(f"max_stored{s}") for s in ("0", "1", "_first")]
        src_gathered = [sem(f"src_gathered{s}") for s in range(SLOTS)]
        gathers_begun, loads_begun = sem("gathers_begun"), sem("loads_begun")
        same_spread, first_turned, ea_turned, src_turned = sem("same_spread"), sem("first_turned"), sem("ea_turned"), sem("src_turned")
        dst_filled = sem("dst_filled")
        hid_summed = [sem("hid_summed0"), sem("hid_summed1")]
        hid_made = [sem("hid_made0"), sem("hid_made1")]
        v_summed, v_copied, max_scanned, max_turned = sem("v_summed"), sem("v_copied"), sem("max_scanned"), sem("max_turned")
        table_padded, table_loaded, table_step, src_padded = sem("table_padded"), sem("table_loaded"), sem("table_step"), sem("src_padded")
        picks_loaded, picks_converted, picks_spread, picks_ready = sem("picks_loaded"), sem("picks_converted"), sem("picks_spread"), sem("picks_ready")
        onehot_made, onehot_used, parts_copied, parts_added, pick_placed = sem("onehot_made"), sem("onehot_used"), sem("parts_copied"), sem("parts_added"), sem("pick_placed")
        carry_loaded, gather_staged, final_step, final_done, out_written = sem("carry_loaded"), sem("gather_staged"), sem("final_step"), sem("final_done"), sem("out_written")
        max_gathered = [sem("max_gathered0"), sem("max_gathered1")]

        def by_group(t):
            return bass.AP(t.tensor, 0, [[S * F, A], [R * F, LANES], [BLK * F, G], [1, R * F]])

        ea_view = by_group(edge_attr)
        first_view = by_group(first_rows)
        src_view = bass.AP(src.tensor, 0, [[S, A], [R, LANES], [BLK, G], [1, R]]).bitcast(U32)
        pick_view = bass.AP(src_pad.tensor, PICK, [[S, A], [R, LANES], [BLK, G + 2 * SLOTS]])
        same_view = bass.AP(same_dram.tensor, 0, [[S, A], [BLK, G], [1, BLK]])
        max_view = run_max[0:A * LEN, :].rearrange("(a g p r) f -> a p g (r f)", a=A, g=G, p=LANES)
        dst_flat = dst.rearrange("(p e) -> p e", p=PN)

        def chunk(a):
            return slice(a * LANES, (a + 1) * LANES)

        block_ = ctx.enter_context(nc.Block())

        ea_rows = ea_in[:, :, :, :].rearrange("p s r f -> p s (r f)")
        first_rows_in = first_in[:, :, :, :].rearrange("p s r f -> p s (r f)")
        max_rows = max_out[:, :, :, :].rearrange("p s r f -> p s (r f)")

        def all_stored(eng):
            for half in range(2):
                eng.wait_ge(max_stored[half], A * D * PAIRS // 2)
            eng.wait_ge(max_stored[2], A * D)

        def all_cleared(eng):
            for c in range(CLEARS_IN_FLIGHT):
                eng.wait_ge(rows_cleared[c], D * len(range(c, ZDMAS, CLEARS_IN_FLIGHT)))

        def halves(eng, to, fr, sem_):
            cut = PN // 16 * 16
            for lo, hi in ((0, cut), (cut, PN)):
                eng.dma_start(to[lo:hi], fr[lo:hi]).then_inc(sem_, D)

        @block_.sync
        def _(sp):
            cleared = first_rows[0:E, :].rearrange("n f -> (n f)").rearrange("(z p c) -> z p c", p=P, c=ZCOL)

            def clear(z0, z1):
                for z in range(z0, z1):
                    wait(sp, rows_cleared[z % CLEARS_IN_FLIGHT], D * (z // CLEARS_IN_FLIGHT))
                    sp.dma_start(cleared[z], zeros[:, :]).then_inc(rows_cleared[z % CLEARS_IN_FLIGHT], D)

            def load(tile, view, loaded, g, count, which, slot):
                for a in range(A):
                    sp.dma_start(tile[chunk(a), slot:slot + count],
                                 view[a, :, bass.ds(g, count), :]).then_inc(loaded[which], D)

            def load_picks(batch):
                for a in range(A):
                    sp.dma_start(pick_i[chunk(a), :], pick_view[a, :, bass.ds(batch * SLOTS + (SLOTS + 1), SLOTS)],
                                 allow_slow_non_contiguous=True).then_inc(picks_loaded, D)

            halves(sp, x_sb, x.rearrange("(p j) f -> p j f", p=PN), x_loaded)
            sp.dma_start(ends_i[:, :], dst.rearrange("(o b e) -> o b e", o=1, e=SEARCH)[:, :, SEARCH - 1],
                         allow_slow_non_contiguous=True).then_inc(ends_loaded, D)
            halves(sp, dst_i, dst_flat, dst_loaded)
            sp.dma_start(before_i[1:PN, :], dst_flat[0:PN - 1, EP - 1:EP],
                         allow_slow_non_contiguous=True).then_inc(dst_loaded, D)
            sp.dma_start(start_ix[:, :], bass.AP(dst.tensor, 0, [[S, A], [1, 1]]).bitcast(U32),
                         allow_slow_non_contiguous=True).then_inc(starts_loaded, D)
            sp.dma_start(start_i[:, :], bass.AP(dst.tensor, S, [[0, PN], [S, A - 1]]),
                         allow_slow_non_contiguous=True).then_inc(starts_loaded, D)
            sp.wait_ge(zeros_made, 1)
            load(src_ix, src_view, ix_loaded, 0, 1, 2, SLOTS - 1)
            load(src_ix, src_view, ix_loaded, 1, 2, 0, 0)
            sp.wait_ge(consts_made, 4)
            for a in range(A):
                for part in range(3):
                    sp.dma_start(w1_blk[a * F:(a + 1) * F, part, a % 2, :], W1[part * F:(part + 1) * F, :]).then_inc(weights_loaded, D)
                sp.dma_start(b2_col[a * F:(a + 1) * F, :], b2.rearrange("(f o) -> f o", o=1)).then_inc(weights_loaded, D)
            for a in range(2):
                sp.dma_start(w2_blk[a * HID:(a + 1) * HID, a, :], W2).then_inc(weights_loaded, D)
                sp.dma_start(b1_col[a * HID:(a + 1) * HID, :], b1.rearrange("(f o) -> f o", o=1)).then_inc(weights_loaded, D)
            clear(0, CLEARED_EARLY)
            sp.wait_ge(h_made, 1)
            halves(sp, h_dram.rearrange("(p j) f -> p j f", p=PN), h_sb, h_written)
            sp.wait_ge(dst_ready, 1)
            halves(sp, dst_dram.rearrange("b e -> (b e)").rearrange("(p e) -> p e", p=PN), dst_16, dst_written)
            sp.wait_ge(same_made, 3)
            halves(sp, same_dram.rearrange("(p e) -> p e", p=PN), same, same_written)
            sp.wait_ge(h_written, 2 * D)
            sp.wait_ge(table_padded, 1)
            full = N // P
            sp.dma_start(table_f[:, 0:full, :], h_dram[0:full * P, :].rearrange("(t p) f -> p t f", p=P)).then_inc(table_loaded, D)
            sp.dma_start(table_f[0:N - full * P, full, :], h_dram[full * P:N, :]).then_inc(table_loaded, D)
            sp.wait_ge(src_padded, 2 * D)
            load_picks(0)
            sp.dma_start(run_max[A * LEN:A * LEN + 1, :], zeros[0:1, 0:F]).then_inc(zero_row_written, D)
            clear(CLEARED_EARLY, 3 * CLEARED_EARLY)
            sp.wait_ge(src_gathered[SLOTS - 1], gathers_by(SLOTS - 1, 0))
            load(src_ix, src_view, ix_loaded, 3, 2, 1, 2)
            clear(3 * CLEARED_EARLY, ZDMAS)
            all_cleared(sp)
            sp.wait_ge(start_rows_read, D)
            sp.dma_start(bass.AP(first_rows.tensor, 0, [[S * F, A], [1, F]]), start_rows[:, :]).then_inc(start_rows_written, D)
            sp.wait_ge(first_made, 3)
            sp.dma_start(nxt[0:PN - 1, NJ - 1:NJ], first[1:PN, 0:1], allow_slow_non_contiguous=True).then_inc(next_shifted, D)
            sp.wait_ge(same_written, 2 * D)

            def load_rows(g, count, which, slot):
                wait(sp, ea_turned, g - SLOTS + count)
                sp.sem_inc(loads_begun, 1)
                load(ea_rows, ea_view, ea_loaded, g, count, which, slot)
                wait(sp, max_scanned, g - SLOTS + count)
                sp.sem_inc(loads_begun, 1)
                sp.dma_start(same_in[:, slot:slot + count, :], same_view[:, bass.ds(g, count), :]).then_inc(same_loaded[which], D)
                load(first_rows_in, first_view, first_loaded, g, count, which, slot)

            def store(g, count, which, slot):
                sp.wait_ge(max_turned, g + count)
                sp.sem_inc(loads_begun, 1)
                for a in range(A):
                    sp.dma_start(max_view[a, :, bass.ds(g, count), :], max_rows[chunk(a), slot:slot + count, :]).then_inc(max_stored[which], D)

            def load_pair(j, half, turn):
                g = j * 2 + 1
                if not isinstance(j, int):
                    for slot in (half * 2, half * 2 + 1):
                        sp.wait_ge(src_gathered[slot], gathers_by(slot, turn - 1))
                        sp.sem_inc(loads_begun, 1)
                    load(src_ix, src_view, ix_loaded, g, 2, half, half * 2)
                load_rows(g, 2, half, half * 2)
                if not isinstance(j, int):
                    store(g - 4, 2, half, half * 2)
                elif j == 1:
                    store(0, 1, 2, SLOTS - 1)
                if half == 1:
                    sp.wait_ge(picks_converted, turn)
                    sp.sem_inc(loads_begun, 1)
                    load_picks(turn)

            def first_group():
                for s in scattered:
                    sp.wait_ge(s, D * HB * NHB // 2)
                load_rows(0, 1, 2, SLOTS - 1)

            over_pairs(sp, first_group, load_pair)
            for j in range(PAIRS - 2, PAIRS):
                store(2 * j + 1, 2, j % 2, j % 2 * 2)
            all_stored(sp)
            sp.dma_start(carry[:, :, :], bass.AP(run_max.tensor, S * F, [[0, PN], [LEN * F, A - 1], [1, F]])).then_inc(carry_loaded, D)
            with sp.Fori(0, NHB // 2) as i:
                sp.wait_ge(final_done, i * 2 + 2)
                cols = bass.ds(i * (2 * HB), 2 * HB)
                sp.dma_start(out.rearrange("(p j) f -> p j f", p=PN)[:, cols, :], out_sb[:, cols, :]).then_inc(out_written, D)
            sp.wait_ge(out_written, D * NHB // 2)

        @block_.gpsimd
        def _(pool):
            pool.memset(zeros[:, :], 0.0).then_inc(zeros_made, 1)
            pool.memset(ident[:, :], 0.0).then_inc(consts_made, 1)
            pool.memset(spread[:, :, :], 0.0).then_inc(consts_made, 1)
            pool.memset(w1_blk[:, :, :, :], 0.0).then_inc(consts_made, 1)
            pool.memset(w2_blk[:, :, :], 0.0).then_inc(consts_made, 1)
            pool.memset(ones[:, :], 1.0).then_inc(numbers_made, 1)
            pool.iota(node_i[:, :], pattern=[[1, NJ]], base=0, channel_multiplier=NJ).then_inc(numbers_made, 1)
            pool.wait_ge(consts_made, 4)
            pool.iota(tile_node_i[:, :], pattern=[[P, TILES]], base=0, channel_multiplier=1).then_inc(numbers_made, 1)
            pool.affine_select(out=ident[:, :], in_=ident[:, :], compare_op=ALU.not_equal, fill=1.0,
                               base=0, pattern=[[-1, P]], channel_multiplier=1).then_inc(numbers_made, 1)
            pool.affine_select(out=spread[:, :, :], in_=spread[:, :, :], compare_op=ALU.not_equal, fill=1.0,
                               base=0, pattern=[[-1, A], [0, F]], channel_multiplier=1).then_inc(numbers_made, 1)

            def gather_group(g, slot, turn):
                pool.wait_ge(ix_loaded[2 if is_first(turn) else slot // 2], (A * D) * (1 if is_first(turn) else turn))
                wait(pool, src_turned, g - SLOTS + 1)
                pool.sem_inc(gathers_begun, 1)
                for r in range(R if isinstance(g, int) else PICK):
                    pool.indirect_dma_start(
                        out=src_in[:, slot, r, :], out_offset=None, in_=h_dram[:, :],
                        in_offset=bass.IndirectOffsetOnAxis(ap=src_ix[:, slot, r:r + 1], axis=0),
                    ).then_inc(src_gathered[slot], D)

            pool.wait_ge(starts_loaded, 2 * D)
            pool.wait_ge(h_written, 2 * D)
            pool.indirect_dma_start(out=start_rows[:, :], out_offset=None, in_=h_dram[:, :],
                                    in_offset=bass.IndirectOffsetOnAxis(ap=start_ix[:, 0:1], axis=0)).then_inc(start_rows_read, D)
            gather_group(0, SLOTS - 1, 0)
            gather_group(1, 0, 1)
            gather_group(2, 1, 1)

            def read_blocks(hb, half):
                pool.wait_ge(search_staged, hb + 1)
                pool.sem_inc(gathers_begun, 1)
                for k in range(HB):
                    pool.indirect_dma_start(
                        out=block_rows[:, half, k, :], out_offset=None, in_=dst_dram[:, :],
                        in_offset=bass.IndirectOffsetOnAxis(ap=search_ix[:, half * HB + k:half * HB + k + 1], axis=0),
                    ).then_inc(blocks_read[half], D)

            pool.wait_ge(dst_written, 2 * D)
            for half in range(2):
                read_blocks(half, half)
            with pool.Fori(1, NHB // 2) as i:
                for half in range(2):
                    read_blocks(i * 2 + half, half)

            gather_group(3, 2, 1)

            pool.wait_ge(start_rows_written, D)
            all_cleared(pool)
            with pool.Fori(0, NHB // 2) as i:
                for half in range(2):
                    pool.wait_ge(scatter_staged, i * 2 + half + 1)
                    pool.sem_inc(gathers_begun, 1)
                    for k in range(HB):
                        pool.indirect_dma_start(
                            out=first_rows[:, :],
                            out_offset=bass.IndirectOffsetOnAxis(ap=scatter_ix[:, half * HB + k:half * HB + k + 1], axis=0),
                            in_=scatter_h[:, half, k, :], in_offset=None,
                        ).then_inc(scattered[half], D)

            gather_group(4, 3, 1)
            with pool.Fori(0, PAIRS // 2 - 1) as i:
                for slot in range(SLOTS):
                    gather_group(i * SLOTS + (SLOTS + 1 + slot), slot, i + 2)

            all_stored(pool)
            pool.wait_ge(zero_row_written, D)
            with pool.Fori(0, NHB // 2) as i:
                for half in range(2):
                    pool.wait_ge(gather_staged, i * 2 + half + 1)
                    pool.sem_inc(gathers_begun, 1)
                    for k in range(HB):
                        pool.indirect_dma_start(
                            out=gathered_max[:, half, k, :], out_offset=None, in_=run_max[:, :],
                            in_offset=bass.IndirectOffsetOnAxis(ap=gather_ix[:, half * HB + k:half * HB + k + 1], axis=0),
                        ).then_inc(max_gathered[half], D)

        @block_.scalar
        def _(act):
            act.dma_start(src_pad[0:E].rearrange("(p e) -> p e", p=P), src.rearrange("(p e) -> p e", p=P)).then_inc(src_padded, D)
            act.wait_ge(zeros_made, 1)
            act.dma_start(src_pad[E:E + PAD].rearrange("(p e) -> p e", p=P), zeros[:, 0:PAD // P].bitcast(I32)).then_inc(src_padded, D)
            act.wait_ge(ends_bcast, 1)
            nc.scalar.copy(ends[:, 0:500], ps_ends[0][0:PN, 0:500]).then_inc(ends_copied, 1)
            nc.scalar.copy(ends[:, 500:BLOCKS], ps_ends[1][0:PN, 0:BLOCKS - 500]).then_inc(ends_copied, 1)
            act.wait_ge(dst_loaded, 3 * D)
            nc.scalar.copy(dst_16[:, :], dst_i[:, :]).then_inc(dst_ready, 1)
            act.wait_ge(ln_step, 7)
            nc.scalar.activation(std[:, :], var[:, :], ACT.Sqrt).then_inc(std_made, 1)

            def count_blocks(j, buf):
                wait(act, coarse_done, j - 1)
                nc.scalar.activation(signs[:, buf, :], ends[:, :], ACT.Sign, bias=below_node[:, bass.ds(j, 1)], scale=-1.0,
                                     accum_out=coarse[:, bass.ds(j, 1)]).then_inc(coarse_done, 1)

            act.wait_ge(node_ready, 2)
            act.wait_ge(ends_copied, 2)
            count_blocks(0, 0)
            count_blocks(1, 1)
            with act.Fori(1, NJ // 2) as i:
                for buf in range(2):
                    count_blocks(i * 2 + buf, buf)
            act.wait_ge(weights_loaded, D * (4 * A + 4))

            def step(g, slot, turn):
                par = (slot + 1) % 2
                act.wait_ge(hid_summed[0], g + 1)
                wait(act, v_summed, g - 1)
                nc.scalar.activation(hid[:, par, 0, :], ps_hid[0][:, :], ACT.Relu, bias=b1_col[:, 0:1]).then_inc(hid_made[0], 1)
                act.wait_ge(v_summed, g + 1)
                wait(act, max_scanned, g - 1)
                nc.scalar.activation(v_t[:, par, :], ps_v[:, :], ACT.Identity, bias=b2_col[:, 0:1]).then_inc(v_copied, 1)
                if slot == SLOTS - 1:
                    if not is_first(turn):
                        act.wait_ge(onehot_used, turn * CHUNKS)
                        wait(act, parts_added, turn - 1)
                        nc.scalar.copy(picked_parts[:, :], ps_parts[0:PARTS * F, :]).then_inc(parts_copied, 1)
                    act.wait_ge(picks_loaded, turn * (A * D) + A * D)
                    wait(act, picks_spread, turn)
                    nc.scalar.copy(pick_f[:, :], pick_i[:, :]).then_inc(picks_converted, 1)
                    act.wait_ge(picks_spread, turn + 1)
                    wait(act, onehot_made, turn * CHUNKS)
                    nc.scalar.copy(pick_all[:, :], ps_all[:, :]).then_inc(picks_ready, 1)

            over_groups(act, step)

        @block_.tensor
        def _(pe):
            pe.wait_ge(numbers_made, 5)
            pe.wait_ge(ends_ready, 1)
            nc.tensor.matmul(ps_ends[0][0:PN, 0:500], ones[0:1, :], ends_f[0:1, 0:500], start=True, stop=True)
            nc.tensor.matmul(ps_ends[1][0:PN, 0:BLOCKS - 500], ones[0:1, :], ends_f[0:1, 500:BLOCKS],
                             start=True, stop=True).then_inc(ends_bcast, 1)
            pe.wait_ge(weights_loaded, D * (4 * A + 4))
            pe.wait_ge(ends_copied, 2)
            pe.wait_ge(table_step, 8)

            def step(g, slot, turn):
                par = (slot + 1) % 2
                which, landed = (2, 1) if is_first(turn) else (slot // 2, turn)
                pe.wait_ge(same_loaded[which], landed * D)
                wait(pe, max_scanned, g - 1)
                nc.tensor.matmul(ps_same[par][:, :], spread[:, :, :].rearrange("k a f -> k (a f)"), same_in[:, slot, :],
                                 start=True, stop=True).then_inc(same_spread, 1)
                if slot == 0 and not isinstance(g, int):
                    pe.wait_ge(parts_copied, turn - 1)
                    for a in range(A):
                        mm = nc.tensor.matmul(ps_pick[chunk(a), 0:SLOTS * LANES], add_parts[:, :],
                                              picked_parts[:, :].rearrange("k (m a l) -> k m a l", m=SLOTS, a=A)[:, :, a, :],
                                              start=True, stop=True)
                    mm.then_inc(parts_added, 1)

                def look_up(place):
                    for m in range(0 if is_first(turn) else PLACES[slot][place]):
                        c = chunk_at(slot, place, m)
                        if c == 0:
                            wait(pe, parts_copied, turn - 1)
                        pe.wait_ge(onehot_made, (turn - 1) * CHUNKS + (c + 1))
                        for t in range(CT):
                            mm = nc.tensor.matmul(ps_parts[0:PARTS * F, :], table[:, c * CT + t, :], onehot[:, c % RING, t, :],
                                                  start=(c + t == 0), stop=(c == CHUNKS - 1 and t == CT - 1))
                        mm.then_inc(onehot_used, 1)

                parts = ((2, ea_t, ea_turned), (1, dst_t, dst_filled), (0, src_t, src_turned))
                for part, t, ready in parts:
                    if part == 0:
                        look_up(0)
                        if not isinstance(g, int):
                            pe.wait_ge(pick_placed, g - SLOTS)
                    pe.wait_ge(ready, g + 1)
                    for q in range(2):
                        if part == 2:
                            wait(pe, hid_made[q], g)
                        rows = slice(q * 2 * F, (q + 1) * 2 * F)
                        mm = nc.tensor.matmul(ps_hid[q][:, :], w1_blk[rows, part, :, :].rearrange("k a h -> k (a h)"),
                                              t[rows, par, :], start=(part == 2), stop=(part == 0))
                        if part == 0:
                            mm.then_inc(hid_summed[q], 1)
                look_up(1)
                wait(pe, v_copied, g)
                for q in range(2):
                    pe.wait_ge(hid_made[q], g + 1)
                    mm = nc.tensor.matmul(ps_v[q * 2 * F:(q + 1) * 2 * F, :], w2_blk[:, :, :].rearrange("k a f -> k (a f)"),
                                          hid[:, par, q, :], start=True, stop=True)
                mm.then_inc(v_summed, 1)
                look_up(2)
                if slot == SLOTS - 1:
                    pe.wait_ge(picks_converted, turn + 1)
                    wait(pe, picks_ready, turn)
                    for m in range(SLOTS):
                        mm = nc.tensor.matmul(ps_all[:, m * P:(m + 1) * P], pick_f[:, m:m + 1].broadcast_to([P, P]), ident[:, :],
                                              start=True, stop=True)
                    mm.then_inc(picks_spread, 1)

            over_groups(pe, step)

        @block_.vector
        def _(dve):
            V = nc.vector
            dve.wait_ge(ends_loaded, D)
            V.tensor_copy(ends_f[:, :], ends_i[:, :]).then_inc(ends_ready, 1)
            dve.wait_ge(x_loaded, 2 * D)
            V.tensor_reduce(mean[:, :], x_sb[:, :, :], AX_X, ALU.add).then_inc(ln_step, 1)
            dve.wait_ge(ln_step, 1)
            V.tensor_scalar(mean[:, :], mean[:, :], 1.0 / F, None, ALU.mult).then_inc(ln_step, 1)
            dve.wait_ge(ln_step, 2)
            V.tensor_tensor(centred, x_sb[:, :, :], mean[:, :].unsqueeze(2).broadcast_to([PN, NJ, F]), ALU.subtract).then_inc(ln_step, 1)
            dve.wait_ge(ln_step, 3)
            V.tensor_tensor(squared, centred, centred, ALU.mult).then_inc(ln_step, 1)
            dve.wait_ge(ln_step, 4)
            V.tensor_reduce(var[:, :], squared, AX_X, ALU.add).then_inc(ln_step, 1)
            dve.wait_ge(ln_step, 5)
            V.tensor_scalar(var[:, :], var[:, :], 1.0 / F, EPS, ALU.mult, ALU.add).then_inc(ln_step, 2)
            dve.wait_ge(std_made, 1)
            V.reciprocal(rstd[:, :], std[:, :]).then_inc(ln_step, 1)
            dve.wait_ge(ln_step, 8)
            V.scalar_tensor_tensor(out=h_sb[:, :, :], in0=centred, scalar=0.0,
                                   in1=rstd[:, :].unsqueeze(2).broadcast_to([PN, NJ, F]),
                                   op0=ALU.max, op1=ALU.mult).then_inc(h_made, 1)
            V.memset(table_f[:, TILES - 1, :], 0.0).then_inc(table_padded, 1)
            dve.wait_ge(numbers_made, 5)
            V.tensor_copy(node[:, :], node_i[:, :]).then_inc(node_ready, 1)
            dve.wait_ge(node_ready, 1)
            V.tensor_scalar(below_node[:, :], node[:, :], -0.5, None, ALU.add).then_inc(node_ready, 1)
            dve.wait_ge(dst_loaded, 3 * D)
            V.memset(before_i[0:1, :], -1).then_inc(same_made, 1)
            V.tensor_tensor(same[:, 1:EP], dst_i[:, 1:EP], dst_i[:, 0:EP - 1], ALU.is_equal).then_inc(same_made, 1)
            dve.wait_ge(same_made, 1)
            V.tensor_tensor(same[:, 0:1], dst_i[:, 0:1], before_i[:, :], ALU.is_equal).then_inc(same_made, 1)

            V.tensor_copy(tile_node[:, :], tile_node_i[:, :])
            for q in range(PARTS):
                V.tensor_copy(add_parts[q * F:(q + 1) * F, :], ident[q * F:(q + 1) * F, q * F:(q + 1) * F]).then_inc(table_step, 1)
            dve.wait_ge(table_loaded, 2 * D)
            for q in range(PARTS):
                part = table[:, :, q * F:(q + 1) * F]
                V.tensor_copy(part, table_f).then_inc(table_step, 1)
                dve.wait_ge(table_step, 4 + 2 * q)
                if q < PARTS - 1:
                    V.tensor_tensor(table_f, table_f, part, ALU.subtract).then_inc(table_step, 1)
                    dve.wait_ge(table_step, 5 + 2 * q)

            def stage_search(hb, half):
                cols = bass.ds(hb * HB, HB)
                dve.wait_ge(coarse_done, hb * HB + HB)
                V.tensor_scalar(ended[:, cols], coarse[:, cols], 0.5, BLOCKS / 2, ALU.mult, ALU.add).then_inc(block_made, 1)
                dve.wait_ge(block_made, hb + 1)
                V.tensor_scalar(search_ix[:, half * HB:(half + 1) * HB], ended[:, cols], float(BLOCKS - 1), None, ALU.min).then_inc(search_staged, 1)

            def count_below(hb, half, landed):
                dve.wait_ge(blocks_read[half], landed)
                for k in range(HB):
                    col = bass.ds(hb * HB + k, 1)
                    if k >= 2:
                        dve.wait_ge(fine_done, hb * HB + (k - 1))
                    V.tensor_scalar(junk[:, k % 2, :], block_rows[:, half, k, :], node[:, col], None, ALU.is_lt, ALU.add,
                                    accum_out=fine[:, col]).then_inc(fine_done, 1)
                dve.wait_ge(fine_done, hb * HB + HB)

            stage_search(0, 0)
            stage_search(1, 1)
            with dve.Fori(0, NHB // 2 - 1) as i:
                for half in range(2):
                    count_below(i * 2 + half, half, i * (D * HB) + D * HB)
                    stage_search(i * 2 + (half + 2), half)
            for half in range(2):
                count_below(NHB - 2 + half, half, D * HB * NHB // 2)

            V.tensor_scalar(block[:, :], ended[:, :], float(BLOCKS - 1), None, ALU.min).then_inc(block_made, 1)
            dve.wait_ge(block_made, NHB + 1)

            V.scalar_tensor_tensor(out=first[:, :], in0=block[:, :], scalar=float(SEARCH), in1=fine[:, :],
                                   op0=ALU.mult, op1=ALU.add).then_inc(first_made, 1)
            V.memset(nxt[:, NJ - 1:NJ], float(E)).then_inc(first_made, 1)
            dve.wait_ge(first_made, 2)
            V.tensor_copy(nxt[:, 0:NJ - 1], first[:, 1:NJ]).then_inc(first_made, 1)
            dve.wait_ge(first_made, 3)
            dve.wait_ge(next_shifted, D)
            V.tensor_tensor(empty[:, :], first[:, :], nxt[:, :], ALU.is_equal).then_inc(place_step, 1)
            V.scalar_tensor_tensor(out=tmp[:, :], in0=node[:, :], scalar=float(E), in1=first[:, :],
                                   op0=ALU.add, op1=ALU.subtract).then_inc(place_step, 1)
            dve.wait_ge(place_step, 2)
            V.tensor_tensor(tmp[:, :], tmp[:, :], empty[:, :], ALU.mult).then_inc(place_step, 1)
            dve.wait_ge(place_step, 3)
            V.tensor_tensor(scatter_at[:, :], tmp[:, :], first[:, :], ALU.add).then_inc(place_step, 1)
            dve.wait_ge(place_step, 4)

            def stage_scatter(hb, half, landed):
                if landed is not None:
                    dve.wait_ge(scattered[half], landed)
                V.tensor_copy(scatter_ix[:, half * HB:(half + 1) * HB], scatter_at[:, bass.ds(hb * HB, HB)]).then_inc(place_step, 1)
                V.tensor_copy(scatter_h[:, half, :, :], h_sb[:, bass.ds(hb * HB, HB), :]).then_inc(scatter_staged, 1)

            stage_scatter(0, 0, None)
            stage_scatter(1, 1, None)
            with dve.Fori(1, NHB // 2) as i:
                for half in range(2):
                    stage_scatter(i * 2 + half, half, i * (D * HB))

            base = 4 + NHB
            dve.wait_ge(place_step, base)
            V.tensor_scalar(last[:, :], nxt[:, :], -1.0, None, ALU.add).then_inc(place_step, 1)
            dve.wait_ge(place_step, base + 1)
            V.tensor_copy(gather_at[:, :], last[:, :]).then_inc(place_step, 1)
            dve.wait_ge(place_step, base + 2)
            for a in range(1, A):
                V.tensor_scalar(tmp[:, :], last[:, :], float(a * S), float(LEN - S), ALU.is_ge, ALU.mult).then_inc(place_step, 1)
                dve.wait_ge(place_step, base + 1 + 2 * a)
                V.tensor_tensor(gather_at[:, :], gather_at[:, :], tmp[:, :], ALU.add).then_inc(place_step, 1)
                dve.wait_ge(place_step, base + 2 + 2 * a)
            base += 2 * A
            V.tensor_scalar(tmp[:, :], gather_at[:, :], -1.0, float(A * LEN), ALU.mult, ALU.add).then_inc(place_step, 1)
            dve.wait_ge(place_step, base + 1)
            V.tensor_tensor(tmp[:, :], tmp[:, :], empty[:, :], ALU.mult).then_inc(place_step, 1)
            dve.wait_ge(place_step, base + 2)
            V.tensor_tensor(gather_at[:, :], gather_at[:, :], tmp[:, :], ALU.add).then_inc(place_step, 1)
            dve.wait_ge(starts_loaded, 2 * D)
            V.tensor_copy(start_node[:, :], start_i[:, :]).then_inc(place_step, 1)
            dve.wait_ge(place_step, base + 4)
            for a in range(A - 1):
                V.tensor_scalar(at_start[:, a, :], node[:, :], start_node[:, a:a + 1], None, ALU.is_equal).then_inc(place_step, 1)
            base += 4 + A - 1
            dve.wait_ge(place_step, base)

            def by_rows(t, par):
                return t[:, par, :].rearrange("p (l r) -> p r l", r=R)

            def step(g, slot, turn):
                par = (slot + 1) % 2
                which, landed = (2, 1) if is_first(turn) else (slot // 2, turn)
                def compare(place):
                    for m in range(0 if is_first(turn) else PLACES[slot][place]):
                        c = chunk_at(slot, place, m)
                        if c == 0:
                            dve.wait_ge(picks_ready, turn)
                        wait(dve, onehot_used, (turn - 1) * CHUNKS + (c + 1 - RING))
                        for t in range(CT):
                            n = c * CT + t
                            last = V.tensor_scalar(onehot[:, c % RING, t, :], pick_all[:, :], tile_node[:, n:n + 1], None, ALU.is_equal)
                        last.then_inc(onehot_made, 1)

                dve.wait_ge(ea_loaded[which], landed * (A * D))
                wait(dve, hid_summed[1], g - 1)
                V.transpose(by_rows(ea_t, par), ea_in[:, slot, :, :]).then_inc(ea_turned, 1)
                def fill_dst():
                    dve.wait_ge(first_loaded[which], landed * (A * D))
                    V.transpose(by_rows(dst_t, par), first_in[:, slot, :, :]).then_inc(first_turned, 1)
                    dve.wait_ge(first_turned, g + 1)
                    dve.wait_ge(same_spread, g + 1)
                    V.tensor_tensor_scan(dst_t[:, par, :], ps_same[par][:, :], dst_t[:, par, :],
                                         0.0 if isinstance(g, int) and g == 0 else dst_t[:, 1 - par, BLK - 1:BLK],
                                         ALU.mult, ALU.max).then_inc(dst_filled, 1)

                def turn_src():
                    turned = R
                    if not isinstance(g, int):
                        turned = PICK
                        dve.wait_ge(parts_added, turn - 1)
                        V.tensor_copy(by_rows(src_t, par)[:, PICK, :], ps_pick[:, slot * LANES:(slot + 1) * LANES]).then_inc(pick_placed, 1)
                    dve.wait_ge(src_gathered[slot], gathers_by(slot, turn))
                    V.transpose(by_rows(src_t, par)[:, 0:turned, :], src_in[:, slot, 0:turned, :]).then_inc(src_turned, 1)

                if isinstance(g, int):
                    turn_src()
                fill_dst()
                compare(0)
                if not isinstance(g, int):
                    turn_src()
                compare(1)
                dve.wait_ge(hid_summed[1], g + 1)
                wait(dve, v_summed, g - 1)
                V.tensor_scalar(hid[:, par, 1, :], ps_hid[1][:, :], b1_col[:, 0:1], 0.0, ALU.add, ALU.max).then_inc(hid_made[1], 1)
                compare(2)
                dve.wait_ge(v_copied, g + 1)
                wait(dve, max_turned, g - 1)
                V.tensor_tensor_scan(max_t[:, par, :], ps_same[par][:, :], v_t[:, par, :],
                                     0.0 if isinstance(g, int) and g == 0 else max_t[:, 1 - par, BLK - 1:BLK],
                                     ALU.mult, ALU.max).then_inc(max_scanned, 1)
                dve.wait_ge(max_scanned, g + 1)
                if not is_first(turn):
                    wait(dve, max_stored[slot // 2], (turn - 1) * (A * D))
                    if isinstance(g, int) and slot == SLOTS - 1:
                        dve.wait_ge(max_stored[2], A * D)
                V.transpose(max_out[:, slot, :, :], by_rows(max_t, par)).then_inc(max_turned, 1)

            dve.wait_ge(weights_loaded, D * (4 * A + 4))
            over_groups(dve, step)

            def stage_gather(hb, half):
                V.tensor_copy(gather_ix[:, half * HB:(half + 1) * HB], gather_at[:, bass.ds(hb * HB, HB)]).then_inc(gather_staged, 1)

            STEPS = 2 * A

            def finish(hb, half, landed):
                cols = bass.ds(hb * HB, HB)
                got = gathered_max[:, half, :, :]
                dve.wait_ge(max_gathered[half], landed)
                n = 0
                for a in range(A - 1):
                    V.tensor_tensor(carry_part[:, :, :], at_start[:, a, cols].unsqueeze(2).broadcast_to([PN, HB, F]),
                                    carry[:, a, :].unsqueeze(1).broadcast_to([PN, HB, F]), ALU.mult).then_inc(final_step, 1)
                    n += 1
                    dve.wait_ge(final_step, hb * (STEPS - 1) + n)
                    V.tensor_tensor(got, got, carry_part[:, :, :], ALU.max).then_inc(final_step, 1)
                    n += 1
                    dve.wait_ge(final_step, hb * (STEPS - 1) + n)
                V.tensor_tensor(got, got, h_sb[:, cols, :], ALU.max).then_inc(final_step, 1)
                n += 1
                dve.wait_ge(final_step, hb * (STEPS - 1) + n)
                V.tensor_tensor(out_sb[:, cols, :], got, x_sb[:, cols, :], ALU.add).then_inc(final_done, 1)
                dve.wait_ge(final_done, hb + 1)

            stage_gather(0, 0)
            stage_gather(1, 1)
            dve.wait_ge(carry_loaded, D)
            with dve.Fori(0, NHB // 2 - 1) as i:
                for half in range(2):
                    finish(i * 2 + half, half, i * (D * HB) + D * HB)
                    stage_gather(i * 2 + (half + 2), half)
            for half in range(2):
                finish(NHB - 2 + half, half, D * HB * NHB // 2)


_INS = ['x', 'src', 'dst', 'edge_attr_32', 'L0_gnn_W1', 'L0_gnn_b1', 'L0_gnn_W2', 'L0_gnn_b2']
_OUTS = [((N, F), 'float32')]


def kernel(**inputs):
    import numpy as _np
    import concourse.bacc as _bacc
    from concourse import mybir as _mybir
    from concourse.bass_utils import run_bass_kernel_spmd as _run

    nc = _bacc.Bacc("TRN2", target_bir_lowering=False, num_devices=1)
    arrays, args = {}, []
    for name in _INS:
        a = _np.ascontiguousarray(inputs[name])
        arrays[f"in_{name}_dram"] = a
        args.append(nc.dram_tensor(f"in_{name}_dram", a.shape, _mybir.dt.from_np(a.dtype), kind="ExternalInput").ap())
    for i, (shape, dtype) in enumerate(_OUTS):
        dt = _mybir.dt.from_np(_np.dtype(dtype))
        args.append(nc.dram_tensor(f"out_{i}_dram", shape, dt, kind="ExternalOutput").ap())
    build(nc, *args)
    r = _run(nc, [arrays], core_ids=[0])
    got = tuple(r.results[0][f"out_{i}_dram"] for i in range(len(_OUTS)))
    return got[0]
```

```python
from contextlib import ExitStack

import concourse.bass as bass
from concourse import mybir

F32, BF16, I16, I32, U32 = mybir.dt.float32, mybir.dt.bfloat16, mybir.dt.int16, mybir.dt.int32, mybir.dt.uint32
ALU = mybir.AluOpType
ACT = mybir.ActivationFunctionType
AX_X = mybir.AxisListType.X

N, E, F, HID = 12500, 400000, 32, 64
EPS = 1e-5
P = 128
A = 4
LANES = P // A
R = 16
BLK = LANES * R
assert LANES == F == 32
G = -(-E // (A * BLK))
while (E - G * BLK) % (A - 1):
    G += 1
LEN = G * BLK
S = (E - LEN) // (A - 1)
assert 0 < S <= LEN and (A - 1) * S + LEN == E

PN, NJ = 125, 100
assert PN * NJ == N
EP = E // PN
SEARCH = 640
BLOCKS = E // SEARCH
assert BLOCKS * SEARCH == E
HB = 5
NHB = NJ // HB

SLOTS = 4
PAIRS = (G - 1) // 2
assert G % 2 == 1 and PAIRS % 2 == 0
PICKS = 2
PARTS = 3
FOLD = 4
TILES = -(-N // (FOLD * P))
CT = 5
CHUNKS = TILES // CT
FOLD_BITS = FOLD.bit_length() - 1
assert CHUNKS * CT == TILES and N % FOLD == 0 and FOLD == 1 << FOLD_BITS and FOLD * F == P
RING = 2
assert PICKS * CHUNKS % RING == 0
PLACES = ((0, 2, 1), (0, 1, 1), (0, 2, 1), (0, 1, 1))
assert sum(map(sum, PLACES)) == PICKS * CHUNKS and PICKS == 2 and sum(map(sum, PLACES[:2])) == CHUNKS
PAD = 2 * SLOTS * BLK
ZCOL = 1000
ZDMAS = E * F // (P * ZCOL)
CLEARS_IN_FLIGHT, CLEARED_EARLY = 3, 4
assert ZDMAS * P * ZCOL == E * F
D = 16


def wait(eng, sem, v):
    if not isinstance(v, int) or v > 0:
        eng.wait_ge(sem, v)


def over_pairs(eng, first_group, pair):
    first_group()
    for half in range(2):
        pair(half, half, 1)
    with eng.Fori(0, PAIRS // 2 - 1) as i:
        for half in range(2):
            pair(i * 2 + (half + 2), half, i + 2)


def over_groups(eng, step):
    def pair(j, half, turn):
        for m in range(2):
            step(j * 2 + (m + 1), half * 2 + m, turn)

    over_pairs(eng, lambda: step(0, SLOTS - 1, 0), pair)


def before(g, slot, turn):
    return g - 1, (slot - 1) % SLOTS, turn - (slot == 0)


LAST = (G - 1, SLOTS - 1, PAIRS // 2)


def is_first(turn):
    return isinstance(turn, int) and turn == 0


def gathers_by(slot, turn):
    full = slot == SLOTS - 1
    if isinstance(turn, int) and turn <= 1:
        return (turn + full) * (R * D)
    return turn * ((R - PICKS) * D) + (PICKS * D + full * R * D)


def chunk_at(slot, place, m):
    return sum(map(sum, PLACES[:slot])) + sum(PLACES[slot][:place]) + m


def build(nc, x, src, dst, edge_attr, W1, b1, W2, b2, out):
    ctx = ExitStack()
    with ctx:
        def sb(name, shape, dt=F32):
            return ctx.enter_context(nc.sbuf_tensor(name, shape, dt))

        def bank(name):
            return ctx.enter_context(nc.psum_tensor(name, [P, 512], F32))

        def sem(name):
            return ctx.enter_context(nc.semaphore(name))

        src_pad = nc.dram_tensor("src_pad", [E + PAD], I32, kind="Internal").ap()
        h_dram = nc.dram_tensor("h_dram", [N, F], F32, kind="Internal").ap()
        dst_dram = nc.dram_tensor("dst_dram", [BLOCKS, SEARCH], I16, kind="Internal").ap()
        same_dram = nc.dram_tensor("same_dram", [E], BF16, kind="Internal").ap()
        first_rows = nc.dram_tensor("first_rows", [E + N, F], F32, kind="Internal").ap()
        run_max = nc.dram_tensor("run_max", [A * LEN + 1, F], F32, kind="Internal").ap()

        x_sb = sb("x_sb", [PN, NJ, F])
        h_sb = sb("h_sb", [PN, NJ, F])
        work_all = sb("work", [P, 2 * NJ * F])
        work = work_all[0:PN, :]
        table_f = work_all[:, NJ * F:NJ * F + TILES * P].rearrange("p (t f) -> p t f", f=P)
        centred = work[:, 0:NJ * F].rearrange("p (j f) -> p j f", f=F)
        squared = work[:, NJ * F:2 * NJ * F].rearrange("p (j f) -> p j f", f=F)
        out_sb = work[:, 0:NJ * F].rearrange("p (j f) -> p j f", f=F)
        mean = sb("mean", [PN, NJ])
        var = sb("var", [PN, NJ])
        std = sb("std", [PN, NJ])
        rstd = sb("rstd", [PN, NJ])
        node_i = sb("node_i", [PN, NJ], I32)
        node = sb("node", [PN, NJ])
        below_node = sb("below_node", [PN, NJ])
        coarse = sb("coarse", [PN, NJ])
        fine = sb("fine", [PN, NJ])
        ended = sb("ended", [PN, NJ])
        block = sb("block", [PN, NJ])
        first = sb("first", [PN, NJ])
        nxt = sb("nxt", [PN, NJ])
        empty = sb("empty", [PN, NJ])
        tmp = sb("tmp", [PN, NJ])
        scatter_at = sb("scatter_at", [PN, NJ])
        last = sb("last", [PN, NJ])
        gather_at = sb("gather_at", [PN, NJ])
        junk = sb("junk", [PN, 2, SEARCH], I16)
        signs = sb("signs", [PN, 2, BLOCKS], BF16)
        ends_i = sb("ends_i", [1, BLOCKS], I32)
        ends_f = sb("ends_f", [1, BLOCKS])
        ends = sb("ends", [PN, BLOCKS])
        search_ix = sb("search_ix", [PN, 2 * HB], U32)
        scatter_ix = sb("scatter_ix", [PN, 2 * HB], U32)
        scatter_h = sb("scatter_h", [PN, 2, HB, F])
        gather_ix = sb("gather_ix", [PN, 2 * HB], U32)
        gathered_max = sb("gathered_max", [PN, 2, HB, F])
        carry_part = sb("carry_part", [PN, HB, F])
        start_ix = sb("start_ix", [A, 1], U32)
        start_rows = sb("start_rows", [A, F])
        start_i = sb("start_i", [PN, A - 1], I32)
        start_node = sb("start_node", [PN, A - 1])
        at_start = sb("at_start", [PN, A - 1, NJ])
        carry = sb("carry", [PN, A - 1, F])

        dst_i = sb("dst_i", [PN, EP], I32)
        dst_16 = sb("dst_16", [PN, EP], I16)
        before_i = sb("before_i", [PN, 1], I32)
        same = sb("same", [PN, EP], BF16)

        table = sb("table", [P, TILES, PARTS, P], BF16)
        column_i = sb("column_i", [P, TILES], I32)
        column = sb("column", [P, TILES])
        fold = sb("fold", [P, 1])
        ident = sb("ident", [P, P])
        add_fold = sb("add_fold", [P, F])
        pick_i = sb("pick_i", [P, SLOTS, PICKS], I32)
        pick_f = sb("pick_f", [P, SLOTS, PICKS])
        pick_all = sb("pick_all", [P, SLOTS * P], I16)
        pick_column = sb("pick_column", [P, SLOTS * P], I16)
        pick_fold = sb("pick_fold", [P, SLOTS * P], I16)
        onehot = sb("onehot", [P, RING, CT, SLOTS * P], BF16)
        picked_rows = sb("picked_rows", [P, PICKS, SLOTS * P])

        ea_in = sb("ea_in", [P, SLOTS, R, F])
        first_in = sb("first_in", [P, SLOTS, R, F])
        block_rows = [t[0:PN].rearrange("p s r f -> p (s r f)").bitcast(I16)[:, 0:HB * SEARCH].rearrange("p (k e) -> p k e", k=HB)
                      for t in (ea_in, first_in)]

        ones = sb("ones", [1, PN])
        spread = sb("spread", [A, A, F], BF16)
        w1_x = sb("w1_x", [P, 2, 2, HID])
        w1_dst = sb("w1_dst", [P, 2, HID])
        w2_blk = sb("w2_blk", [P, 2, F])
        b1_col = sb("b1_col", [P, 1])
        b2_col = sb("b2_col", [P, 1])

        src_in = sb("src_in", [P, SLOTS, R, F])
        same_in = sb("same_in", [A, SLOTS, BLK], BF16)
        src_ix = sb("src_ix", [P, SLOTS, R], U32)
        x_t = sb("x_t", [P, 2, 2, BLK])
        dst_t = sb("dst_t", [P, 2, BLK])
        hid = sb("hid", [P, 2, 2, BLK])
        zeros = hid[:, :, :, :].rearrange("p b q e -> p (b q e)")[:, 0:ZCOL]
        v_t = sb("v_t", [P, 2, BLK])
        max_t = sb("max_t", [P, 2, BLK])
        max_out = sb("max_out", [P, SLOTS + 1, R, F])

        ps_same = [bank("ps_same0"), bank("ps_same1")]
        ps_hid = [bank("ps_hid0"), bank("ps_hid1")]
        ps_v = bank("ps_v")
        ps_all, ps_rows, ps_pick = bank("ps_all"), bank("ps_rows"), bank("ps_pick")
        ps_ends = [ps_rows, ps_pick]

        x_loaded, dst_loaded, ends_loaded = sem("x_loaded"), sem("dst_loaded"), sem("ends_loaded")
        weights_loaded, starts_loaded = sem("weights_loaded"), sem("starts_loaded")
        h_written, dst_written, same_written = sem("h_written"), sem("dst_written"), sem("same_written")
        rows_cleared = [sem(f"rows_cleared{c}") for c in range(CLEARS_IN_FLIGHT)]
        zero_row_written, start_rows_read, start_rows_written = sem("zero_row_written"), sem("start_rows_read"), sem("start_rows_written")
        next_shifted = sem("next_shifted")
        zeros_made, consts_made, numbers_made = sem("zeros_made"), sem("consts_made"), sem("numbers_made")
        ln_step, std_made, h_made = sem("ln_step"), sem("std_made"), sem("h_made")
        node_ready = sem("node_ready")
        dst_ready, same_made, ends_ready, ends_bcast, ends_copied = sem("dst_ready"), sem("same_made"), sem("ends_ready"), sem("ends_bcast"), sem("ends_copied")
        block_made = sem("block_made")
        coarse_done, search_staged, fine_done = sem("coarse_done"), sem("search_staged"), sem("fine_done")
        blocks_read = [sem("blocks_read0"), sem("blocks_read1")]
        place_step, first_made = sem("place_step"), sem("first_made")
        scatter_staged = sem("scatter_staged")
        scattered = [sem("scattered0"), sem("scattered1")]
        ea_loaded = [sem(f"ea_loaded{s}") for s in ("0", "1", "_first")]
        first_loaded = [sem(f"first_loaded{s}") for s in ("0", "1", "_first")]
        same_loaded = [sem(f"same_loaded{s}") for s in ("0", "1", "_first")]
        ix_loaded = [sem(f"ix_loaded{s}") for s in ("0", "1", "_first")]
        max_stored = [sem(f"max_stored{s}") for s in ("0", "1", "_first")]
        src_gathered = [sem(f"src_gathered{s}") for s in range(SLOTS)]
        gathers_begun, loads_begun = sem("gathers_begun"), sem("loads_begun")
        same_spread, first_turned, ea_turned, src_turned = sem("same_spread"), sem("first_turned"), sem("ea_turned"), sem("src_turned")
        dst_filled = sem("dst_filled")
        hid_summed = [sem("hid_summed0"), sem("hid_summed1")]
        hid_made = [sem("hid_made0"), sem("hid_made1")]
        v_summed, v_copied, max_scanned, max_turned = sem("v_summed"), sem("v_copied"), sem("max_scanned"), sem("max_turned")
        table_padded, table_loaded, table_step, src_padded = sem("table_padded"), sem("table_loaded"), sem("table_step"), sem("src_padded")
        picks_loaded, picks_converted, picks_spread, picks_ready = sem("picks_loaded"), sem("picks_converted"), sem("picks_spread"), sem("picks_ready")
        picks_split, onehot_made, onehot_used = sem("picks_split"), sem("onehot_made"), sem("onehot_used")
        rows_masked, rows_added, pick_placed = sem("rows_masked"), sem("rows_added"), sem("pick_placed")
        carry_loaded, gather_staged, final_step, final_done, out_written = sem("carry_loaded"), sem("gather_staged"), sem("final_step"), sem("final_done"), sem("out_written")
        max_gathered = [sem("max_gathered0"), sem("max_gathered1")]

        def by_group(t):
            return bass.AP(t.tensor, 0, [[S * F, A], [R * F, LANES], [BLK * F, G], [1, R * F]])

        ea_view = by_group(edge_attr)
        first_view = by_group(first_rows)
        src_view = bass.AP(src.tensor, 0, [[S, A], [R, LANES], [BLK, G], [1, R]]).bitcast(U32)
        padded_src_view = bass.AP(src_pad.tensor, 0, [[S, A], [R, LANES], [BLK, G + 2], [1, R]]).bitcast(U32)
        pick_view = bass.AP(src_pad.tensor, R - PICKS, [[S, A], [R, LANES], [BLK, G + 2 * SLOTS], [1, PICKS]])
        same_view = bass.AP(same_dram.tensor, 0, [[S, A], [BLK, G], [1, BLK]])
        max_view = run_max[0:A * LEN, :].rearrange("(a g p r) f -> a p g (r f)", a=A, g=G, p=LANES)
        dst_flat = dst.rearrange("(p e) -> p e", p=PN)

        def chunk(a):
            return slice(a * LANES, (a + 1) * LANES)

        block_ = ctx.enter_context(nc.Block())

        ea_rows = ea_in[:, :, :, :].rearrange("p s r f -> p s (r f)")
        first_rows_in = first_in[:, :, :, :].rearrange("p s r f -> p s (r f)")
        max_rows = max_out[:, :, :, :].rearrange("p s r f -> p s (r f)")

        def all_stored(eng):
            for half in range(2):
                eng.wait_ge(max_stored[half], A * D * PAIRS // 2)
            eng.wait_ge(max_stored[2], A * D)

        def all_cleared(eng):
            for c in range(CLEARS_IN_FLIGHT):
                eng.wait_ge(rows_cleared[c], D * len(range(c, ZDMAS, CLEARS_IN_FLIGHT)))

        def halves(eng, to, fr, sem_):
            cut = PN // 16 * 16
            for lo, hi in ((0, cut), (cut, PN)):
                eng.dma_start(to[lo:hi], fr[lo:hi]).then_inc(sem_, D)

        @block_.sync
        def _(sp):
            cleared = first_rows[0:E, :].rearrange("n f -> (n f)").rearrange("(z p c) -> z p c", p=P, c=ZCOL)

            def clear(z0, z1):
                for z in range(z0, z1):
                    wait(sp, rows_cleared[z % CLEARS_IN_FLIGHT], D * (z // CLEARS_IN_FLIGHT))
                    sp.dma_start(cleared[z], zeros[:, :]).then_inc(rows_cleared[z % CLEARS_IN_FLIGHT], D)

            def load(tile, view, loaded, g, count, which, slot, turned=0):
                for a in range(A):
                    sp.dma_start(tile[chunk((a + turned) % A), slot:slot + count],
                                 view[a, :, bass.ds(g, count), :]).then_inc(loaded[which], D)

            def load_picks(ahead):
                for a in range(A):
                    sp.dma_start(pick_i[chunk(a)], pick_view[a, :, bass.ds(ahead * SLOTS + (SLOTS + 1), SLOTS), :]).then_inc(picks_loaded, D)

            halves(sp, x_sb, x.rearrange("(p j) f -> p j f", p=PN), x_loaded)
            sp.dma_start(ends_i[:, :], dst.rearrange("(o b e) -> o b e", o=1, e=SEARCH)[:, :, SEARCH - 1],
                         allow_slow_non_contiguous=True).then_inc(ends_loaded, D)
            halves(sp, dst_i, dst_flat, dst_loaded)
            sp.dma_start(before_i[1:PN, :], dst_flat[0:PN - 1, EP - 1:EP],
                         allow_slow_non_contiguous=True).then_inc(dst_loaded, D)
            sp.dma_start(start_ix[:, :], bass.AP(dst.tensor, 0, [[S, A], [1, 1]]).bitcast(U32),
                         allow_slow_non_contiguous=True).then_inc(starts_loaded, D)
            sp.dma_start(start_i[:, :], bass.AP(dst.tensor, S, [[0, PN], [S, A - 1]]),
                         allow_slow_non_contiguous=True).then_inc(starts_loaded, D)
            sp.wait_ge(zeros_made, 1)
            load(src_ix, src_view, ix_loaded, 0, 1, 2, SLOTS - 1)
            load(src_ix, src_view, ix_loaded, 1, 2, 0, 0)
            sp.wait_ge(consts_made, 5)
            w1_src, w1_node, w1_edge = W1[0:F, :], W1[F:2 * F, :], W1[2 * F:3 * F, :]
            for a in range(A):
                for q in range(2):
                    sp.dma_start(w1_x[chunk(a), q, a % 2, :], w1_src if a // 2 == q else w1_edge).then_inc(weights_loaded, D)
                sp.dma_start(w1_dst[chunk(a), a % 2, :], w1_node).then_inc(weights_loaded, D)
                sp.dma_start(b2_col[a * F:(a + 1) * F, :], b2.rearrange("(f o) -> f o", o=1)).then_inc(weights_loaded, D)
            for a in range(2):
                sp.dma_start(w2_blk[a * HID:(a + 1) * HID, a, :], W2).then_inc(weights_loaded, D)
                sp.dma_start(b1_col[a * HID:(a + 1) * HID, :], b1.rearrange("(f o) -> f o", o=1)).then_inc(weights_loaded, D)
            sp.wait_ge(dst_ready, 1)
            halves(sp, dst_dram.rearrange("b e -> (b e)").rearrange("(p e) -> p e", p=PN), dst_16, dst_written)
            clear(0, CLEARED_EARLY)
            sp.wait_ge(h_made, 1)
            halves(sp, h_dram.rearrange("(p j) f -> p j f", p=PN), h_sb, h_written)
            sp.wait_ge(same_made, 3)
            halves(sp, same_dram.rearrange("(p e) -> p e", p=PN), same, same_written)
            sp.wait_ge(h_written, 2 * D)
            sp.wait_ge(table_padded, 1)
            full = N // (FOLD * P)
            h_columns = h_dram.rearrange("(c q) f -> c (q f)", q=FOLD)
            sp.dma_start(table_f[:, 0:full, :], h_columns[0:full * P, :].rearrange("(t p) f -> p t f", p=P)).then_inc(table_loaded, D)
            sp.dma_start(table_f[0:N // FOLD - full * P, full, :], h_columns[full * P:N // FOLD, :]).then_inc(table_loaded, D)
            sp.wait_ge(src_padded, 2 * D)
            load_picks(0)
            sp.dma_start(run_max[A * LEN:A * LEN + 1, :], zeros[0:1, 0:F]).then_inc(zero_row_written, D)
            clear(CLEARED_EARLY, 3 * CLEARED_EARLY)
            sp.wait_ge(src_gathered[SLOTS - 1], gathers_by(SLOTS - 1, 0))
            load(src_ix, src_view, ix_loaded, 3, 2, 1, 2)
            clear(3 * CLEARED_EARLY, ZDMAS)
            all_cleared(sp)
            sp.wait_ge(start_rows_read, D)
            sp.dma_start(bass.AP(first_rows.tensor, 0, [[S * F, A], [1, F]]), start_rows[:, :]).then_inc(start_rows_written, D)
            sp.wait_ge(first_made, 3)
            sp.dma_start(nxt[0:PN - 1, NJ - 1:NJ], first[1:PN, 0:1], allow_slow_non_contiguous=True).then_inc(next_shifted, D)
            sp.wait_ge(same_written, 2 * D)

            def load_rows(g, count, which, slot):
                wait(sp, ea_turned, (g - SLOTS + count) * 2)
                sp.sem_inc(loads_begun, 1)
                load(ea_rows, ea_view, ea_loaded, g, count, which, slot, turned=A // 2)
                if isinstance(g, int) and g == 0:
                    for s in scattered:
                        sp.wait_ge(s, D * HB * NHB // 2)
                wait(sp, max_scanned, g - SLOTS + count)
                sp.sem_inc(loads_begun, 1)
                sp.dma_start(same_in[:, slot:slot + count, :], same_view[:, bass.ds(g, count), :]).then_inc(same_loaded[which], D)
                load(first_rows_in, first_view, first_loaded, g, count, which, slot)

            def store(g, count, which, slot):
                sp.wait_ge(max_turned, g + count)
                sp.sem_inc(loads_begun, 1)
                for a in range(A):
                    sp.dma_start(max_view[a, :, bass.ds(g, count), :], max_rows[chunk(a), slot:slot + count, :]).then_inc(max_stored[which], D)

            def load_indices(g, half, turn):
                for slot in (half * 2, half * 2 + 1):
                    sp.wait_ge(src_gathered[slot], gathers_by(slot, turn - 1))
                    sp.sem_inc(loads_begun, 1)
                load(src_ix, padded_src_view, ix_loaded, g, 2, half, half * 2)

            def load_pair(j, half, turn):
                g = j * 2 + 1
                load_rows(g, 2, half, half * 2)
                if not isinstance(j, int):
                    load_indices(g + 2, 1 - half, turn + half)
                    store(g - 4, 2, half, half * 2)
                if half == 1:
                    sp.wait_ge(picks_converted, turn)
                    sp.sem_inc(loads_begun, 1)
                    load_picks(turn)

            load_indices(5, 0, 2)

            over_pairs(sp, lambda: load_rows(0, 1, 2, SLOTS - 1), load_pair)
            store(0, 1, 2, SLOTS)
            for j in range(PAIRS - 2, PAIRS):
                store(2 * j + 1, 2, j % 2, j % 2 * 2)
            all_stored(sp)
            sp.dma_start(carry[:, :, :], bass.AP(run_max.tensor, S * F, [[0, PN], [LEN * F, A - 1], [1, F]])).then_inc(carry_loaded, D)
            with sp.Fori(0, NHB // 2) as i:
                sp.wait_ge(final_done, i * 2 + 2)
                cols = bass.ds(i * (2 * HB), 2 * HB)
                sp.dma_start(out.rearrange("(p j) f -> p j f", p=PN)[:, cols, :], out_sb[:, cols, :]).then_inc(out_written, D)
            sp.wait_ge(out_written, D * NHB // 2)
            sp.wait_ge(ix_loaded[0], A * D * (PAIRS // 2 + 1))

        @block_.gpsimd
        def _(pool):
            pool.memset(zeros[:, :], 0.0).then_inc(zeros_made, 1)
            pool.memset(ident[:, :], 0.0).then_inc(consts_made, 1)
            pool.memset(spread[:, :, :], 0.0).then_inc(consts_made, 1)
            pool.memset(w1_x[:, :, :, :], 0.0).then_inc(consts_made, 1)
            pool.memset(w1_dst[:, :, :], 0.0).then_inc(consts_made, 1)
            pool.memset(w2_blk[:, :, :], 0.0).then_inc(consts_made, 1)
            pool.memset(ones[:, :], 1.0).then_inc(numbers_made, 1)
            pool.iota(node_i[:, :], pattern=[[1, NJ]], base=0, channel_multiplier=NJ).then_inc(numbers_made, 1)
            pool.wait_ge(consts_made, 5)
            pool.iota(column_i[:, :], pattern=[[P, TILES]], base=0, channel_multiplier=1).then_inc(numbers_made, 1)
            pool.affine_select(out=ident[:, :], in_=ident[:, :], compare_op=ALU.not_equal, fill=1.0,
                               base=0, pattern=[[-1, P]], channel_multiplier=1).then_inc(numbers_made, 1)
            pool.affine_select(out=spread[:, :, :], in_=spread[:, :, :], compare_op=ALU.not_equal, fill=1.0,
                               base=0, pattern=[[-1, A], [0, F]], channel_multiplier=1).then_inc(numbers_made, 1)

            def gather_group(g, slot, turn):
                pool.wait_ge(ix_loaded[2 if is_first(turn) else slot // 2], (A * D) * (1 if is_first(turn) else turn))
                wait(pool, src_turned, (g - SLOTS + 1) * 2)
                pool.sem_inc(gathers_begun, 1)
                for r in range(R if isinstance(g, int) else R - PICKS):
                    pool.indirect_dma_start(
                        out=src_in[:, slot, r, :], out_offset=None, in_=h_dram[:, :],
                        in_offset=bass.IndirectOffsetOnAxis(ap=src_ix[:, slot, r:r + 1], axis=0),
                    ).then_inc(src_gathered[slot], D)


            def read_blocks(hb, half):
                pool.wait_ge(search_staged, hb + 1)
                pool.sem_inc(gathers_begun, 1)
                for k in range(HB):
                    pool.indirect_dma_start(
                        out=block_rows[half][:, k, :], out_offset=None, in_=dst_dram[:, :],
                        in_offset=bass.IndirectOffsetOnAxis(ap=search_ix[:, half * HB + k:half * HB + k + 1], axis=0),
                    ).then_inc(blocks_read[half], D)

            pool.wait_ge(dst_written, 2 * D)
            for half in range(2):
                read_blocks(half, half)
            pool.wait_ge(starts_loaded, 2 * D)
            pool.wait_ge(h_written, 2 * D)
            pool.indirect_dma_start(out=start_rows[:, :], out_offset=None, in_=h_dram[:, :],
                                    in_offset=bass.IndirectOffsetOnAxis(ap=start_ix[:, 0:1], axis=0)).then_inc(start_rows_read, D)
            gather_group(0, SLOTS - 1, 0)
            gather_group(1, 0, 1)
            gather_group(2, 1, 1)

            with pool.Fori(1, NHB // 2) as i:
                for half in range(2):
                    read_blocks(i * 2 + half, half)

            gather_group(3, 2, 1)

            pool.wait_ge(start_rows_written, D)
            all_cleared(pool)
            with pool.Fori(0, NHB // 2) as i:
                for half in range(2):
                    pool.wait_ge(scatter_staged, i * 2 + half + 1)
                    pool.sem_inc(gathers_begun, 1)
                    for k in range(HB):
                        pool.indirect_dma_start(
                            out=first_rows[:, :],
                            out_offset=bass.IndirectOffsetOnAxis(ap=scatter_ix[:, half * HB + k:half * HB + k + 1], axis=0),
                            in_=scatter_h[:, half, k, :], in_offset=None,
                        ).then_inc(scattered[half], D)

            gather_group(4, 3, 1)
            with pool.Fori(0, PAIRS // 2 - 1) as i:
                for slot in range(SLOTS):
                    gather_group(i * SLOTS + (SLOTS + 1 + slot), slot, i + 2)

            all_stored(pool)
            pool.wait_ge(zero_row_written, D)
            with pool.Fori(0, NHB // 2) as i:
                for half in range(2):
                    pool.wait_ge(gather_staged, i * 2 + half + 1)
                    pool.sem_inc(gathers_begun, 1)
                    for k in range(HB):
                        pool.indirect_dma_start(
                            out=gathered_max[:, half, k, :], out_offset=None, in_=run_max[:, :],
                            in_offset=bass.IndirectOffsetOnAxis(ap=gather_ix[:, half * HB + k:half * HB + k + 1], axis=0),
                        ).then_inc(max_gathered[half], D)

        @block_.scalar
        def _(act):
            act.wait_ge(ends_bcast, 1)
            nc.scalar.copy(ends[:, 0:500], ps_ends[0][0:PN, 0:500]).then_inc(ends_copied, 1)
            nc.scalar.copy(ends[:, 500:BLOCKS], ps_ends[1][0:PN, 0:BLOCKS - 500]).then_inc(ends_copied, 1)
            def count_blocks(j, buf):
                wait(act, coarse_done, j - 1)
                nc.scalar.activation(signs[:, buf, :], ends[:, :], ACT.Sign, bias=below_node[:, bass.ds(j, 1)], scale=-1.0,
                                     accum_out=coarse[:, bass.ds(j, 1)]).then_inc(coarse_done, 1)

            act.wait_ge(node_ready, 2)
            act.wait_ge(ends_copied, 2)
            count_blocks(0, 0)
            count_blocks(1, 1)
            act.wait_ge(dst_loaded, 3 * D)
            nc.scalar.copy(dst_16[:, :], dst_i[:, :]).then_inc(dst_ready, 1)
            act.dma_start(src_pad[0:E].rearrange("(p e) -> p e", p=P), src.rearrange("(p e) -> p e", p=P)).then_inc(src_padded, D)
            act.wait_ge(zeros_made, 1)
            act.dma_start(src_pad[E:E + PAD].rearrange("(p e) -> p e", p=P), zeros[:, 0:PAD // P].bitcast(I32)).then_inc(src_padded, D)
            with act.Fori(1, HB) as i:
                for buf in range(2):
                    count_blocks(i * 2 + buf, buf)
            act.wait_ge(ln_step, 7)
            nc.scalar.activation(std[:, :], var[:, :], ACT.Sqrt).then_inc(std_made, 1)
            with act.Fori(HB, NJ // 2) as i:
                for buf in range(2):
                    count_blocks(i * 2 + buf, buf)
            act.wait_ge(weights_loaded, D * (4 * A + 4))

            def step(g, slot, turn):
                par = (slot + 1) % 2
                if not isinstance(g, int):
                    act.wait_ge(rows_added, turn - 1)
                    act.wait_ge(hid_summed[1], g - 1)
                    for q in range(2):
                        half = slice(q * P // 2, (q + 1) * P // 2)
                        nc.scalar.copy(x_t[half, par, q, :].rearrange("p (l r) -> p r l", r=R)[:, R - PICKS:R, :],
                                       ps_pick[half, 0:PICKS * SLOTS * LANES].rearrange("p (k m l) -> p k m l", k=PICKS, m=SLOTS)[:, :, slot, :]
                                       ).then_inc(pick_placed, 1)
                act.wait_ge(hid_summed[0], g + 1)
                wait(act, v_summed, g - 1)
                nc.scalar.activation(hid[:, par, 0, :], ps_hid[0][:, :], ACT.Relu, bias=b1_col[:, 0:1]).then_inc(hid_made[0], 1)
                act.wait_ge(v_summed, g + 1)
                wait(act, max_scanned, g - 1)
                nc.scalar.activation(v_t[:, par, :], ps_v[:, :], ACT.Identity, bias=b2_col[:, 0:1]).then_inc(v_copied, 1)
                if slot % 2:
                    batch = turn * 2 - (slot == 1)
                    if slot == SLOTS - 1:
                        act.wait_ge(picks_loaded, turn * (A * D) + A * D)
                        wait(act, picks_spread, batch)
                        nc.scalar.copy(pick_f[:, :, :], pick_i[:, :, :]).then_inc(picks_converted, 1)
                    act.wait_ge(picks_spread, batch + 1)
                    wait(act, picks_split, batch * 2)
                    nc.scalar.copy(pick_all[:, :], ps_all[:, :]).then_inc(picks_ready, 1)

            over_groups(act, step)

        @block_.tensor
        def _(pe):
            pe.wait_ge(numbers_made, 5)
            pe.wait_ge(ends_ready, 1)
            nc.tensor.matmul(ps_ends[0][0:PN, 0:500], ones[0:1, :], ends_f[0:1, 0:500], start=True, stop=True)
            nc.tensor.matmul(ps_ends[1][0:PN, 0:BLOCKS - 500], ones[0:1, :], ends_f[0:1, 500:BLOCKS],
                             start=True, stop=True).then_inc(ends_bcast, 1)
            pe.wait_ge(weights_loaded, D * (4 * A + 4))
            pe.wait_ge(ends_copied, 2)
            pe.wait_ge(table_step, 1 + 2 * FOLD + 2 * PARTS - 1)

            def look_up(slot, turn, place):
                for m in range(0 if is_first(turn) else PLACES[slot][place]):
                    n = chunk_at(slot, place, m)
                    k, c = n // CHUNKS, n % CHUNKS
                    if c == 0:
                        wait(pe, rows_masked, turn * 2 - (2 - k))
                    pe.wait_ge(onehot_made, (turn - 1) * (PICKS * CHUNKS) + (n + 1))
                    for t in range(CT):
                        for part in range(PARTS):
                            mm = nc.tensor.matmul(ps_rows[:, :], table[:, c * CT + t, part, :], onehot[:, n % RING, t, :],
                                                  start=(c + t + part == 0),
                                                  stop=(c == CHUNKS - 1 and t == CT - 1 and part == PARTS - 1))
                    mm.then_inc(onehot_used, 1)

            def layer_two(g, slot, turn, ahead=True):
                par = (slot + 1) % 2
                if ahead:
                    look_up(slot, turn, 1)
                wait(pe, v_copied, g)
                for q in range(2):
                    pe.wait_ge(hid_made[q], g + 1)
                    mm = nc.tensor.matmul(ps_v[q * 2 * F:(q + 1) * 2 * F, :], w2_blk[:, :, :].rearrange("k a f -> k (a f)"),
                                          hid[:, par, q, :], start=True, stop=True)
                mm.then_inc(v_summed, 1)
                if ahead:
                    look_up(slot, turn, 2)
                if slot % 2:
                    k = (slot + 1) // 2 % 2
                    batch = turn * 2 - (slot == 1)
                    pe.wait_ge(picks_converted, turn + (1 - k))
                    wait(pe, picks_ready, batch)
                    for m in range(SLOTS):
                        mm = nc.tensor.matmul(ps_all[:, m * P:(m + 1) * P], pick_f[:, m, k:k + 1].broadcast_to([P, P]), ident[:, :],
                                              start=True, stop=True)
                    mm.then_inc(picks_spread, 1)

            def step(g, slot, turn):
                par = (slot + 1) % 2
                which, landed = (2, 1) if is_first(turn) else (slot // 2, turn)
                pe.wait_ge(same_loaded[which], landed * D)
                wait(pe, max_scanned, g - 1)
                nc.tensor.matmul(ps_same[par][:, :], spread[:, :, :].rearrange("k a f -> k (a f)"), same_in[:, slot, :],
                                 start=True, stop=True).then_inc(same_spread, 1)
                if not is_first(turn):
                    layer_two(*before(g, slot, turn))
                pe.wait_ge(dst_filled, g + 1)
                for q in range(2):
                    wait(pe, hid_made[q], g)
                    rows = slice(q * 2 * F, (q + 1) * 2 * F)
                    nc.tensor.matmul(ps_hid[q][:, :], w1_dst[rows, :, :].rearrange("k a h -> k (a h)"), dst_t[rows, par, :],
                                     start=True, stop=False)
                if slot == 0 and not isinstance(g, int):
                    pe.wait_ge(rows_masked, turn * 2 - 2)
                    for k in range(PICKS):
                        for a in range(A):
                            mm = nc.tensor.matmul(ps_pick[chunk(a), k * SLOTS * LANES:(k + 1) * SLOTS * LANES], add_fold[:, :],
                                                  picked_rows[:, k, :].rearrange("k (m a l) -> k m a l", m=SLOTS, a=A)[:, :, a, :],
                                                  start=True, stop=True)
                    mm.then_inc(rows_added, 1)
                look_up(slot, turn, 0)
                pe.wait_ge(ea_turned, 2 * g + 2)
                if not isinstance(g, int):
                    pe.wait_ge(pick_placed, (g - SLOTS) * 2)
                pe.wait_ge(src_turned, 2 * g + 2)
                for q in range(2):
                    nc.tensor.matmul(ps_hid[q][:, :], w1_x[:, q, :, :].rearrange("k a h -> k (a h)"), x_t[:, par, q, :],
                                     start=False, stop=True).then_inc(hid_summed[q], 1)

            over_groups(pe, step)
            layer_two(*LAST, ahead=False)

        @block_.vector
        def _(dve):
            V = nc.vector
            dve.wait_ge(ends_loaded, D)
            V.tensor_copy(ends_f[:, :], ends_i[:, :]).then_inc(ends_ready, 1)
            dve.wait_ge(numbers_made, 5)
            V.tensor_copy(node[:, :], node_i[:, :]).then_inc(node_ready, 1)
            dve.wait_ge(node_ready, 1)
            V.tensor_scalar(below_node[:, :], node[:, :], -0.5, None, ALU.add).then_inc(node_ready, 1)

            def stage_search(hb, half):
                cols = bass.ds(hb * HB, HB)
                dve.wait_ge(coarse_done, hb * HB + HB)
                V.tensor_scalar(ended[:, cols], coarse[:, cols], 0.5, BLOCKS / 2, ALU.mult, ALU.add).then_inc(block_made, 1)
                dve.wait_ge(block_made, hb + 1)
                V.tensor_scalar(search_ix[:, half * HB:(half + 1) * HB], ended[:, cols], float(BLOCKS - 1), None, ALU.min).then_inc(search_staged, 1)

            dve.wait_ge(x_loaded, 2 * D)
            V.tensor_reduce(mean[:, :], x_sb[:, :, :], AX_X, ALU.add).then_inc(ln_step, 1)
            dve.wait_ge(ln_step, 1)
            V.tensor_scalar(mean[:, :], mean[:, :], 1.0 / F, None, ALU.mult).then_inc(ln_step, 1)
            dve.wait_ge(ln_step, 2)
            V.tensor_tensor(centred, x_sb[:, :, :], mean[:, :].unsqueeze(2).broadcast_to([PN, NJ, F]), ALU.subtract).then_inc(ln_step, 1)
            dve.wait_ge(ln_step, 3)
            V.tensor_tensor(squared, centred, centred, ALU.mult).then_inc(ln_step, 1)
            dve.wait_ge(ln_step, 4)
            V.tensor_reduce(var[:, :], squared, AX_X, ALU.add).then_inc(ln_step, 1)
            dve.wait_ge(ln_step, 5)
            V.tensor_scalar(var[:, :], var[:, :], 1.0 / F, EPS, ALU.mult, ALU.add).then_inc(ln_step, 2)
            stage_search(0, 0)
            stage_search(1, 1)
            dve.wait_ge(std_made, 1)
            V.reciprocal(rstd[:, :], std[:, :]).then_inc(ln_step, 1)
            dve.wait_ge(ln_step, 8)
            V.scalar_tensor_tensor(out=h_sb[:, :, :], in0=centred, scalar=0.0,
                                   in1=rstd[:, :].unsqueeze(2).broadcast_to([PN, NJ, F]),
                                   op0=ALU.max, op1=ALU.mult).then_inc(h_made, 1)
            V.memset(table_f[:, TILES - 1, :], 0.0).then_inc(table_padded, 1)
            dve.wait_ge(dst_loaded, 3 * D)
            V.memset(before_i[0:1, :], -1).then_inc(same_made, 1)
            V.tensor_tensor(same[:, 1:EP], dst_i[:, 1:EP], dst_i[:, 0:EP - 1], ALU.is_equal).then_inc(same_made, 1)
            dve.wait_ge(same_made, 1)
            V.tensor_tensor(same[:, 0:1], dst_i[:, 0:1], before_i[:, :], ALU.is_equal).then_inc(same_made, 1)

            V.tensor_copy(column[:, :], column_i[:, :]).then_inc(table_step, 1)
            for q in range(FOLD):
                V.memset(fold[q * F:(q + 1) * F, :], float(q)).then_inc(table_step, 1)
                V.tensor_copy(add_fold[q * F:(q + 1) * F, :], ident[q * F:(q + 1) * F, q * F:(q + 1) * F]).then_inc(table_step, 1)
            dve.wait_ge(table_loaded, 2 * D)
            for part in range(PARTS):
                V.tensor_copy(table[:, :, part, :], table_f).then_inc(table_step, 1)
                dve.wait_ge(table_step, 2 + 2 * FOLD + 2 * part)
                if part < PARTS - 1:
                    V.tensor_tensor(table_f, table_f, table[:, :, part, :], ALU.subtract).then_inc(table_step, 1)
                    dve.wait_ge(table_step, 3 + 2 * FOLD + 2 * part)

            def count_below(hb, half, landed):
                dve.wait_ge(blocks_read[half], landed)
                for k in range(HB):
                    col = bass.ds(hb * HB + k, 1)
                    if k >= 2:
                        dve.wait_ge(fine_done, hb * HB + (k - 1))
                    V.tensor_scalar(junk[:, k % 2, :], block_rows[half][:, k, :], node[:, col], None, ALU.is_lt, ALU.add,
                                    accum_out=fine[:, col]).then_inc(fine_done, 1)
                dve.wait_ge(fine_done, hb * HB + HB)

            with dve.Fori(0, NHB // 2 - 1) as i:
                for half in range(2):
                    count_below(i * 2 + half, half, i * (D * HB) + D * HB)
                    stage_search(i * 2 + (half + 2), half)
            for half in range(2):
                count_below(NHB - 2 + half, half, D * HB * NHB // 2)

            V.tensor_scalar(block[:, :], ended[:, :], float(BLOCKS - 1), None, ALU.min).then_inc(block_made, 1)
            dve.wait_ge(block_made, NHB + 1)

            V.scalar_tensor_tensor(out=first[:, :], in0=block[:, :], scalar=float(SEARCH), in1=fine[:, :],
                                   op0=ALU.mult, op1=ALU.add).then_inc(first_made, 1)
            V.memset(nxt[:, NJ - 1:NJ], float(E)).then_inc(first_made, 1)
            dve.wait_ge(first_made, 2)
            V.tensor_copy(nxt[:, 0:NJ - 1], first[:, 1:NJ]).then_inc(first_made, 1)
            dve.wait_ge(first_made, 3)
            dve.wait_ge(next_shifted, D)
            V.tensor_tensor(empty[:, :], first[:, :], nxt[:, :], ALU.is_equal).then_inc(place_step, 1)
            V.scalar_tensor_tensor(out=tmp[:, :], in0=node[:, :], scalar=float(E), in1=first[:, :],
                                   op0=ALU.add, op1=ALU.subtract).then_inc(place_step, 1)
            dve.wait_ge(place_step, 2)
            V.tensor_tensor(tmp[:, :], tmp[:, :], empty[:, :], ALU.mult).then_inc(place_step, 1)
            dve.wait_ge(place_step, 3)
            V.tensor_tensor(scatter_at[:, :], tmp[:, :], first[:, :], ALU.add).then_inc(place_step, 1)
            dve.wait_ge(place_step, 4)

            def stage_scatter(hb, half, landed):
                if landed is not None:
                    dve.wait_ge(scattered[half], landed)
                V.tensor_copy(scatter_ix[:, half * HB:(half + 1) * HB], scatter_at[:, bass.ds(hb * HB, HB)]).then_inc(place_step, 1)
                V.tensor_copy(scatter_h[:, half, :, :], h_sb[:, bass.ds(hb * HB, HB), :]).then_inc(scatter_staged, 1)

            stage_scatter(0, 0, None)
            stage_scatter(1, 1, None)
            with dve.Fori(1, NHB // 2) as i:
                for half in range(2):
                    stage_scatter(i * 2 + half, half, i * (D * HB))

            base = 4 + NHB
            dve.wait_ge(place_step, base)
            V.tensor_scalar(last[:, :], nxt[:, :], -1.0, None, ALU.add).then_inc(place_step, 1)
            dve.wait_ge(place_step, base + 1)
            V.tensor_copy(gather_at[:, :], last[:, :]).then_inc(place_step, 1)
            dve.wait_ge(place_step, base + 2)
            for a in range(1, A):
                V.tensor_scalar(tmp[:, :], last[:, :], float(a * S), float(LEN - S), ALU.is_ge, ALU.mult).then_inc(place_step, 1)
                dve.wait_ge(place_step, base + 1 + 2 * a)
                V.tensor_tensor(gather_at[:, :], gather_at[:, :], tmp[:, :], ALU.add).then_inc(place_step, 1)
                dve.wait_ge(place_step, base + 2 + 2 * a)
            base += 2 * A
            V.tensor_scalar(tmp[:, :], gather_at[:, :], -1.0, float(A * LEN), ALU.mult, ALU.add).then_inc(place_step, 1)
            dve.wait_ge(place_step, base + 1)
            V.tensor_tensor(tmp[:, :], tmp[:, :], empty[:, :], ALU.mult).then_inc(place_step, 1)
            dve.wait_ge(place_step, base + 2)
            V.tensor_tensor(gather_at[:, :], gather_at[:, :], tmp[:, :], ALU.add).then_inc(place_step, 1)
            dve.wait_ge(starts_loaded, 2 * D)
            V.tensor_copy(start_node[:, :], start_i[:, :]).then_inc(place_step, 1)
            dve.wait_ge(place_step, base + 4)
            for a in range(A - 1):
                V.tensor_scalar(at_start[:, a, :], node[:, :], start_node[:, a:a + 1], None, ALU.is_equal).then_inc(place_step, 1)
            base += 4 + A - 1
            dve.wait_ge(place_step, base)

            def by_rows(t):
                return t.rearrange("p (l r) -> p r l", r=R)

            def compare(slot, turn, place):
                for m in range(0 if is_first(turn) else PLACES[slot][place]):
                    n = chunk_at(slot, place, m)
                    k, c = n // CHUNKS, n % CHUNKS
                    if c == 0:
                        batch = turn * 2 - (2 - k)
                        dve.wait_ge(picks_ready, batch + 1)
                        wait(dve, rows_masked, batch)
                        V.tensor_scalar(pick_column[:, :], pick_all[:, :], FOLD_BITS, None, ALU.logical_shift_right).then_inc(picks_split, 1)
                        V.tensor_scalar(pick_fold[:, :], pick_all[:, :], FOLD - 1, None, ALU.bitwise_and).then_inc(picks_split, 1)
                        dve.wait_ge(picks_split, batch * 2 + 2)
                    wait(dve, onehot_used, (turn - 1) * (PICKS * CHUNKS) + (n + 1 - RING))
                    for t in range(CT):
                        compared = V.tensor_scalar(onehot[:, n % RING, t, :], pick_column[:, :], column[:, c * CT + t:c * CT + t + 1],
                                                   None, ALU.is_equal)
                    compared.then_inc(onehot_made, 1)

            def mask_rows(batch, k):
                dve.wait_ge(onehot_used, batch * CHUNKS + CHUNKS)
                V.scalar_tensor_tensor(out=picked_rows[:, k, :], in0=pick_fold[:, :], scalar=fold[:, 0:1], in1=ps_rows[:, :],
                                       op0=ALU.is_equal, op1=ALU.mult).then_inc(rows_masked, 1)

            def find_max(g, slot, turn, ahead=True):
                par = (slot + 1) % 2
                if ahead:
                    compare(slot, turn, 2)
                dve.wait_ge(v_copied, g + 1)
                wait(dve, max_turned, g - 1)
                V.tensor_tensor_scan(max_t[:, par, :], ps_same[par][:, :], v_t[:, par, :],
                                     0.0 if isinstance(g, int) and g == 0 else max_t[:, 1 - par, BLK - 1:BLK],
                                     ALU.mult, ALU.max).then_inc(max_scanned, 1)
                dve.wait_ge(max_scanned, g + 1)
                V.transpose(max_out[:, SLOTS if is_first(turn) else slot, :, :], by_rows(max_t[:, par, :])).then_inc(max_turned, 1)

            def step(g, slot, turn):
                par = (slot + 1) % 2
                which, landed = (2, 1) if is_first(turn) else (slot // 2, turn)
                wait(dve, hid_summed[1], g - 1)
                dve.wait_ge(src_gathered[slot], gathers_by(slot, turn))
                turned = R if isinstance(g, int) else R - PICKS
                for q in range(2):
                    half = slice(q * P // 2, (q + 1) * P // 2)
                    V.transpose(by_rows(x_t[half, par, q, :])[:, 0:turned, :], src_in[half, slot, 0:turned, :]).then_inc(src_turned, 1)
                dve.wait_ge(ea_loaded[which], landed * (A * D))
                for q in range(2):
                    half = slice((1 - q) * P // 2, (2 - q) * P // 2)
                    V.transpose(by_rows(x_t[half, par, q, :]), ea_in[half, slot, :, :]).then_inc(ea_turned, 1)
                dve.wait_ge(first_loaded[which], landed * (A * D))
                V.transpose(by_rows(dst_t[:, par, :]), first_in[:, slot, :, :]).then_inc(first_turned, 1)
                dve.wait_ge(first_turned, g + 1)
                dve.wait_ge(same_spread, g + 1)
                V.tensor_tensor_scan(dst_t[:, par, :], ps_same[par][:, :], dst_t[:, par, :],
                                     0.0 if isinstance(g, int) and g == 0 else dst_t[:, 1 - par, BLK - 1:BLK],
                                     ALU.mult, ALU.max).then_inc(dst_filled, 1)
                if not is_first(turn):
                    find_max(*before(g, slot, turn))
                if slot == 0 and not isinstance(g, int):
                    mask_rows(turn * 2 - 3, 1)
                if slot == 2 and not is_first(turn):
                    wait(dve, rows_added, turn - 1)
                    mask_rows(turn * 2 - 2, 0)
                compare(slot, turn, 0)
                compare(slot, turn, 1)
                if not is_first(turn):
                    wait(dve, max_stored[slot // 2], (turn - 1) * (A * D))
                dve.wait_ge(hid_summed[1], g + 1)
                wait(dve, v_summed, g - 1)
                V.tensor_scalar(hid[:, par, 1, :], ps_hid[1][:, :], b1_col[:, 0:1], 0.0, ALU.add, ALU.max).then_inc(hid_made[1], 1)

            dve.wait_ge(weights_loaded, D * (4 * A + 4))
            over_groups(dve, step)
            find_max(*LAST, ahead=False)

            def stage_gather(hb, half):
                V.tensor_copy(gather_ix[:, half * HB:(half + 1) * HB], gather_at[:, bass.ds(hb * HB, HB)]).then_inc(gather_staged, 1)

            STEPS = 2 * A

            def finish(hb, half, landed):
                cols = bass.ds(hb * HB, HB)
                got = gathered_max[:, half, :, :]
                dve.wait_ge(max_gathered[half], landed)
                n = 0
                for a in range(A - 1):
                    V.tensor_tensor(carry_part[:, :, :], at_start[:, a, cols].unsqueeze(2).broadcast_to([PN, HB, F]),
                                    carry[:, a, :].unsqueeze(1).broadcast_to([PN, HB, F]), ALU.mult).then_inc(final_step, 1)
                    n += 1
                    dve.wait_ge(final_step, hb * (STEPS - 1) + n)
                    V.tensor_tensor(got, got, carry_part[:, :, :], ALU.max).then_inc(final_step, 1)
                    n += 1
                    dve.wait_ge(final_step, hb * (STEPS - 1) + n)
                V.tensor_tensor(got, got, h_sb[:, cols, :], ALU.max).then_inc(final_step, 1)
                n += 1
                dve.wait_ge(final_step, hb * (STEPS - 1) + n)
                V.tensor_tensor(out_sb[:, cols, :], got, x_sb[:, cols, :], ALU.add).then_inc(final_done, 1)
                dve.wait_ge(final_done, hb + 1)

            stage_gather(0, 0)
            stage_gather(1, 1)
            dve.wait_ge(carry_loaded, D)
            with dve.Fori(0, NHB // 2 - 1) as i:
                for half in range(2):
                    finish(i * 2 + half, half, i * (D * HB) + D * HB)
                    stage_gather(i * 2 + (half + 2), half)
            for half in range(2):
                finish(NHB - 2 + half, half, D * HB * NHB // 2)


_INS = ['x', 'src', 'dst', 'edge_attr_32', 'L0_gnn_W1', 'L0_gnn_b1', 'L0_gnn_W2', 'L0_gnn_b2']
_OUTS = [((N, F), 'float32')]


def kernel(**inputs):
    import numpy as _np
    import concourse.bacc as _bacc
    from concourse import mybir as _mybir
    from concourse.bass_utils import run_bass_kernel_spmd as _run

    nc = _bacc.Bacc("TRN2", target_bir_lowering=False, num_devices=1)
    arrays, args = {}, []
    for name in _INS:
        a = _np.ascontiguousarray(inputs[name])
        arrays[f"in_{name}_dram"] = a
        args.append(nc.dram_tensor(f"in_{name}_dram", a.shape, _mybir.dt.from_np(a.dtype), kind="ExternalInput").ap())
    for i, (shape, dtype) in enumerate(_OUTS):
        dt = _mybir.dt.from_np(_np.dtype(dtype))
        args.append(nc.dram_tensor(f"out_{i}_dram", shape, dt, kind="ExternalOutput").ap())
    build(nc, *args)
    r = _run(nc, [arrays], core_ids=[0])
    got = tuple(r.results[0][f"out_{i}_dram"] for i in range(len(_OUTS)))
    return got[0]
```
